# Optimizing a Trainium2 kernel written in Bass

```python
import numpy as np
import jax
import jax.numpy as jnp

def _softmax(x, axis=-1):
    return jax.nn.softmax(x, axis=axis)

def _gelu(x):
    return jax.nn.gelu(x, approximate=True)

def _silu(x):
    return jax.nn.silu(x)

def _sigmoid(x):
    return jax.nn.sigmoid(x)

def _layernorm(x, axis=-1, eps=1e-05):
    m = jnp.mean(x, axis=axis, keepdims=True)
    v = jnp.var(x, axis=axis, keepdims=True)
    return (x - m) / jnp.sqrt(v + eps)

def _scatter_add(tgt, idx, src, axis=0):
    return tgt.at[idx].add(src)

def _segment_sum(src, seg, n):
    return jax.ops.segment_sum(src, seg, n)
kernel_name = 'mk_adj_preln_d2_adj_r2_c6cd6e'

def setup_inputs(seed: int=0):
    np.random.seed(seed)
    _w = jnp.asarray

    def _rec_inputs():
        import jax
        import jax.numpy as jnp
        _gk = jax.random.key(seed)
        x = -0.0005207 + 1.001 * jax.random.normal(jax.random.fold_in(_gk, 1), (8192, 128), jnp.float32)
        _w = (1.0 + jnp.arange(8192, dtype=jnp.float32)) ** (-0.5)
        _w = _w / _w.mean()
        _pij = jnp.clip(0.00195312 * _w[:, None] * _w[None, :], 0.0, 1.0)
        _a = jax.random.uniform(jax.random.fold_in(_gk, 2), (8192, 8192)) < _pij
        adj = _a.astype(jnp.int32)
        return (x, adj)
    x, adj = _rec_inputs()

    def _L0_gnn_setup():
        import jax, jax.numpy as jnp
        import numpy as np
        N, IN_DIM, OUT_DIM, HEADS = (4096, 128, 128, 2)
        C = OUT_DIM // HEADS
        ALPHA = 0.2
        NEG = -9000000000000000.0
        key = jax.random.key(seed)
        ks = jax.random.split(key, 9)
        h = jax.random.normal(ks[0], (N, IN_DIM), dtype=jnp.float32)
        adj = jax.random.randint(ks[1], (N, N), 0, 2, dtype=jnp.int32)

        def xav(k, shape):
            fan_in, fan_out = (shape[1], shape[0])
            s = 1.414 * np.sqrt(6.0 / (fan_in + fan_out))
            return jax.random.uniform(k, shape, jnp.float32, -s, s)
        W1 = xav(ks[2], (HEADS * C, IN_DIM))
        W2 = xav(ks[3], (HEADS * C, IN_DIM))
        W3 = xav(ks[4], (HEADS * C, IN_DIM))
        b1 = jnp.zeros((HEADS * C,), jnp.float32)
        b2 = jnp.zeros((HEADS * C,), jnp.float32)
        b3 = jnp.zeros((HEADS * C,), jnp.float32)
        sa = 1.414 * np.sqrt(6.0 / (HEADS + 2 * C))
        a = jax.random.uniform(ks[5], (HEADS, 2 * C), jnp.float32, -sa, sa)
        return {'h': h, 'adj': adj, 'W1': W1, 'b1': b1, 'W2': W2, 'b2': b2, 'W3': W3, 'b3': b3, 'a': a}
    _L0_gnn_all = _L0_gnn_setup()
    _L0_gnn_in = {k: v for k, v in _L0_gnn_all.items() if k in ('W1', 'b1', 'W2', 'b2', 'W3', 'b3', 'a')}
    del _L0_gnn_all

    def _L1_gnn_setup():
        import jax, jax.numpy as jnp
        import numpy as np
        N, IN_C, OUT_C, H = (2048, 128, 128, 8)
        HD = OUT_C // H
        key = jax.random.key(seed)
        k1, k2, k3, k4, k5, k6 = jax.random.split(key, 6)
        node_features = jax.random.normal(k1, (N, IN_C), dtype=jnp.float32)
        adjacency_matrix = jax.random.randint(k2, (N, N), 0, 2, dtype=jnp.int32)
        W_w = jax.random.normal(k3, (OUT_C, IN_C), dtype=jnp.float32) * (1.0 / np.sqrt(IN_C))
        W_b = jax.random.normal(k4, (OUT_C,), dtype=jnp.float32) * 0.01
        a_w = jax.random.normal(k5, (1, 2 * HD), dtype=jnp.float32) * (1.0 / np.sqrt(2 * HD))
        a_b = jax.random.normal(k6, (1,), dtype=jnp.float32) * 0.01
        return {'node_features': node_features, 'adjacency_matrix': adjacency_matrix, 'W_w': W_w, 'W_b': W_b, 'a_w': a_w, 'a_b': a_b}
    _L1_gnn_all = _L1_gnn_setup()
    _L1_gnn_in = {k: v for k, v in _L1_gnn_all.items() if k in ('W_w', 'W_b', 'a_w', 'a_b')}
    del _L1_gnn_all
    return {'x': x, 'adj': adj, 'L0_gnn_W1': _L0_gnn_in['W1'], 'L0_gnn_b1': _L0_gnn_in['b1'], 'L0_gnn_W2': _L0_gnn_in['W2'], 'L0_gnn_b2': _L0_gnn_in['b2'], 'L0_gnn_W3': _L0_gnn_in['W3'], 'L0_gnn_b3': _L0_gnn_in['b3'], 'L0_gnn_a': _L0_gnn_in['a'], 'L1_gnn_W_w': _L1_gnn_in['W_w'], 'L1_gnn_W_b': _L1_gnn_in['W_b'], 'L1_gnn_a_w': _L1_gnn_in['a_w'], 'L1_gnn_a_b': _L1_gnn_in['a_b']}

def reference(x, adj, L0_gnn_W1, L0_gnn_b1, L0_gnn_W2, L0_gnn_b2, L0_gnn_W3, L0_gnn_b3, L0_gnn_a, L1_gnn_W_w, L1_gnn_W_b, L1_gnn_a_w, L1_gnn_a_b):
    import jax
    import jax.numpy as jnp

    def _L0_gnn_ref(h, adj, W1, b1, W2, b2, W3, b3, a):
        import jax, jax.numpy as jnp
        import numpy as np
        N, IN_DIM, OUT_DIM, HEADS = (4096, 128, 128, 2)
        C = OUT_DIM // HEADS
        ALPHA = 0.2
        NEG = -9000000000000000.0
        n = h.shape[0]
        W1h = (h @ W1.T + b1).reshape(n, HEADS, C)
        W2h = (h @ W2.T + b2).reshape(n, HEADS, C)
        W3h = (h @ W3.T + b3).reshape(n, HEADS, C)
        a1, a2 = (a[:, :C], a[:, C:])
        s1 = jnp.einsum('nhc,hc->nh', W1h, a1)
        s2 = jnp.einsum('nhc,hc->nh', W2h, a2)
        e = jax.nn.leaky_relu(s1[:, None, :] + s2[None, :, :], ALPHA)
        e = jnp.where(adj[:, :, None] == 1, e, NEG)
        att = jax.nn.softmax(e, axis=1)
        h_prime = jnp.einsum('ijh,jhc->ihc', att, W3h)
        return h_prime.reshape(n, HEADS * C)

    def _L1_gnn_ref(node_features, adjacency_matrix, W_w, W_b, a_w, a_b):
        import jax, jax.numpy as jnp
        import numpy as np
        N, IN_C, OUT_C, H = (2048, 128, 128, 8)
        HD = OUT_C // H
        n = node_features.shape[0]
        h = node_features @ W_w.T + W_b
        h_heads = h.reshape(n, H, HD)
        w_src = a_w[0, :HD]
        w_dst = a_w[0, HD:]
        s_src = jnp.einsum('nhd,d->hn', h_heads, w_src)
        s_dst = jnp.einsum('nhd,d->hn', h_heads, w_dst)
        scores = s_src[:, :, None] + s_dst[:, None, :] + a_b[0]
        scores = jax.nn.leaky_relu(scores, negative_slope=0.2)
        scores = jnp.where(adjacency_matrix[None, :, :] == 0, jnp.float32(-1000000000.0), scores)
        attn = jax.nn.softmax(scores, axis=-1)
        h_agg = jnp.einsum('hij,jhd->ihd', attn, h_heads)
        h_out = h_agg.reshape(n, OUT_C)
        h_out = h_out + node_features
        return jax.nn.elu(h_out)
    h = jnp.maximum(_layernorm(x, axis=-1), 0.0)
    x = x + _L0_gnn_ref(h, adj, L0_gnn_W1, L0_gnn_b1, L0_gnn_W2, L0_gnn_b2, L0_gnn_W3, L0_gnn_b3, L0_gnn_a)
    h = jnp.maximum(_layernorm(x, axis=-1), 0.0)
    x = x + _L1_gnn_ref(h, adj, L1_gnn_W_w, L1_gnn_W_b, L1_gnn_a_w, L1_gnn_a_b)
    return x

_drawn_inputs = setup_inputs


def setup_inputs(seed=0):
    import zlib

    import numpy as np

    out = dict(_drawn_inputs(seed))
    spreads = {'L0_gnn_b1': (0.0, 0.8), 'L0_gnn_b2': (0.0, 0.8), 'L0_gnn_b3': (0.0, 0.1)}
    factors = {'L1_gnn_W_b': 8.0}
    for name, (base, spread) in spreads.items():
        noise = np.random.default_rng([zlib.crc32(name.encode()), seed]).standard_normal(out[name].shape)
        drawn = base * np.exp(spread * noise) if base else spread * noise
        out[name] = jnp.asarray(drawn.astype(out[name].dtype))
    for name, factor in factors.items():
        out[name] = (out[name] * factor).astype(out[name].dtype)
    return out
```

```python
from contextlib import ExitStack

import concourse.bass as bass
from concourse import mybir

P = 128
D = 128
CH = 512
IB = CH // P
EPS = 1e-5
SLOPE = 0.2
STEEP = float(2 ** 30)
H0, HD0 = 2, 64
H1, HD1 = 8, 16
K0 = HD0 + 1
K1 = HD1 + 1
PARTS = 3
JP = 4
JQ = 8
GJ0 = 2
GJ1 = 4
SLOTS = 4
AHEAD = 2
LATE = 5
HS = 4


def gat_kernel(nc, x, adj, W1, b1, W2, b2, W3, W3T, b3, a, Ww, WwT, Wb, aw, ab, ident_in, sel_in, out):
    f32, bf16, fp8, i32, u8 = mybir.dt.float32, mybir.dt.bfloat16, mybir.dt.float8e4, mybir.dt.int32, mybir.dt.uint8
    ALU, ACT, AX = mybir.AluOpType, mybir.ActivationFunctionType, mybir.AxisListType
    N = x.shape[0]
    NB = N // P
    NCH = N // CH
    NP0 = NB // JP
    NP1 = NB // JQ
    NG0 = NB // GJ0
    NG1 = NB // GJ1
    XW = max(H0 * 2 * PARTS * K0, H1 * 2 * PARTS * K1)

    ctx = ExitStack()
    with ctx:
        ctx.enter_context(nc.allow_non_contiguous_dma(reason="small weight vectors"))

        def sb(name, shape, dt):
            return ctx.enter_context(nc.sbuf_tensor(name, shape, dt))

        def sem(name):
            return ctx.enter_context(nc.semaphore(name))

        def scratch(name, shape, dt):
            return nc.dram_tensor(name, shape, dt, kind="Internal").ap()

        s1_rows = [scratch("s1_rows0", [H0, N], f32), scratch("s1_rows1", [H1, N], f32)]
        adjT8 = scratch("adjT8", [NCH, NP0, P, JP * CH], u8)
        x1_dram = scratch("x1_dram", [N, D], f32)
        h1_dram = scratch("h1_dram", [N, D], f32)
        agg_dram = scratch("agg_dram", [N, D], f32)

        Xt = sb("Xt", [P, NB * XW], bf16)
        ident = sb("ident", [P, P], f32)
        ones = sb("ones", [P, CH], f32)
        sel = sb("sel", [P, 4, 2 * K1], f32)
        minus1 = sb("minus1", [P, NB], f32)
        minus_half = sb("minus_half", [P, NB], f32)
        thr = sb("thr", [P, NB, H1], f32)
        steep_s2 = sb("steep_s2", [P, NB, H1], f32)
        Ai = sb("Ai", [P, NB, H1], f32)
        Ci = sb("Ci", [P, NB, H1], f32)
        Smax = sb("Smax", [P, 2, H1], f32)
        sumV = sb("sumV", [P, H1 * K1 if H1 * K1 > H0 * K0 else H0 * K0], f32)
        wcat = sb("wcat", [P, 128 + 2 * H1], f32)
        brow = sb("brow", [1, 128 + 2 * H1], f32)
        WORK = 22016
        work = sb("work", [P, WORK], f32)

        class Region:
            def __init__(self, base, size, view):
                self.at, self.end, self.view = base, size, view

            def take(self, dt, *dims):
                n = 1
                for d in dims:
                    n *= d
                words = n * {f32: 4, bf16: 2, fp8: 1}[dt] // 4
                v = self.view[:, self.at:self.at + words]
                self.at += words
                assert self.at <= self.end, (self.at, self.end)
                if dt != f32:
                    v = v.bitcast(dt)
                if len(dims) > 1:
                    names = "abcde"[:len(dims)]
                    v = v.rearrange(f"p ({' '.join(names)}) -> p {' '.join(names)}",
                                    **{m: d for m, d in zip(names[1:], dims[1:])})
                return v

        r = Region(0, WORK, work)
        hT = r.take(f32, NB * P)
        tail = r.at
        x_all = r.take(f32, NB, D)
        r.at = tail
        V32 = r.take(f32, NB, 128 + 2 * H1)
        bexp = r.take(f32, NB, H1, 2)
        zrow = r.take(f32, NB, H1)
        mrow = r.take(f32, NB, H1)
        stat = r.take(f32, 2, NB)
        xr = Region(0, NB * XW // 2, Xt[:, :].bitcast(f32))
        sq = xr.take(f32, NB, D)
        s1_sb = xr.take(f32, N)
        wn = [xr.take(f32, D), xr.take(f32, D)]
        ablk = [xr.take(f32, H1), xr.take(f32, H1)]
        bcol = [xr.take(f32, 1), xr.take(f32, 1)]
        abrow = xr.take(f32, H1)
        XG = 4
        r2 = Region(0, NB * P, work)
        xf = [r2.take(f32, XG * XW // PARTS) for _ in range(2)]
        r = Region(0, WORK, work)
        nat = [r.take(bf16, IB, JP * P) for _ in range(SLOTS)]
        adjT = [r.take(bf16, JP, CH) for _ in range(SLOTS)]
        mplus = [[r.take(bf16, GJ0, CH) for _ in range(H0)] for _ in range(SLOTS)]
        mminus = [[r.take(bf16, GJ0, CH) for _ in range(H0)] for _ in range(SLOTS)]
        small = [r.take(fp8, JP, CH) for _ in range(2)]
        s1bc0 = r.take(f32, H0, CH)
        stage0 = r.take(f32, IB, H0, 2 * PARTS * K0)
        r = Region(0, WORK, work)
        adj8 = [r.take(fp8, JQ, CH) for _ in range(SLOTS)]
        mask8 = [[r.take(fp8, GJ1, CH) for _ in range(HS)] for _ in range(SLOTS)]
        s1bcA = r.take(f32, 2, CH)
        s1bcD = r.take(f32, 2, CH)
        stage1 = r.take(f32, 6, CH)
        comb = r.take(f32, IB, HS, 2 * K1)
        ep = r.take(f32, IB * HS, K1)
        ep2 = r.take(f32, IB * HS, K1)
        flag1 = r.take(f32, IB * HS)
        rec1 = r.take(f32, IB * HS)
        agg_sb = r.take(f32, IB * HS, HD1)
        w0 = sb("w0", [P, H0, PARTS * K0], f32)
        flag0 = sb("flag0", [P, H0], f32)
        rec0 = sb("rec0", [P, H0], f32)
        x1_sb = sb("x1_sb", [P, IB, D], f32)
        x_in = sb("x_in", [P, IB, D], f32)
        FB = NB // 8 if NB >= 32 else NB // 4
        NF = NB // FB
        r = Region(0, WORK, work)
        fin_y = [r.take(f32, FB, D) for _ in range(2)]
        fin_h = [r.take(f32, FB, D) for _ in range(2)]
        fin_x = [r.take(f32, FB, D) for _ in range(2)]
        fin_e = [r.take(f32, FB, D) for _ in range(2)]

        bank = [ctx.enter_context(nc.psum_tensor(f"bank{i}", [P, 512], f32)) for i in range(8)]

        def bc(ap, n):
            return ap.unsqueeze(len(ap.shape)).to_broadcast([*ap.shape, n])

        block = ctx.enter_context(nc.Block())
        sync, act, dve, pe, pool = nc.sync, nc.scalar, nc.vector, nc.tensor, nc.gpsimd
        phase_end = sem("phase_end")

        passed = {id(e): sem(f"passed_{n}") for n, e in (("sp", sync), ("act", act), ("dve", dve), ("pe", pe), ("pool", pool))}

        def wait_alone(eng, s, value):
            eng.wait_ge(s, value)
            eng.sem_inc(passed[id(eng)], 1)

        def phase_over(eng, k):
            eng.drain().then_inc(phase_end, 1)
            eng.wait_ge(phase_end, 5 * k)

        xv = x.rearrange("(b p) d -> p b d", p=P)
        x1v = x1_dram.rearrange("(b p) d -> p b d", p=P)
        h1v = h1_dram.rearrange("(b p) d -> p b d", p=P)
        LG = 4
        LB = NB // LG

        class Prologue:
            def __init__(self, layer):
                self.l, self.s = layer, {}
                self.H, self.HD = (H0, HD0) if layer == 0 else (H1, HD1)
                self.K = self.HD + 1
                for name in ("w_in", "const_in", "x_arrived", "sum_done", "centred", "squared", "var_done",
                             "rstd_done", "h_done", "hT_in_psum", "u_in_psum", "u_copied",
                             "b_in_psum", "b_copied", "v_in_psum", "s1_in_psum", "s1_copied",
                             "s1_stored", "local_max", "global_max", "shifted", "b_exp", "ac_ready", "ac_exp",
                             "sumv_in_psum", "xf_ready", "hi_done", "rest1", "mid_done", "lo_done",
                             "dve_step", "h_stored", "consts"):
                    self.s[name] = sem(f"l{layer}_{name}")
                self.x_in = [sem(f"l{layer}_x_in{g}") for g in range(LG)]
                self.VW = 128 + 2 * self.H
                self.n_t = NB // 4
                self.n_v = NB // 2
                self.n_s = N // 512
                self.groups = NB // XG

                for name in ("hT_copied", "v_copied", "s1_copied"):
                    self.s[name] = [sem(f"l{layer}_{name}_{e}") for e in ("act", "dve")]

            def views(self):
                H, K = self.H, self.K
                vw = V32[:, :, 0:self.VW]
                return vw[:, :, 0:128], vw[:, :, 128:128 + H], vw[:, :, 128 + H:128 + 2 * H]

        def copied(eng, sems, n):
            for who in range(2):
                if (n + 1 - who) // 2:
                    eng.wait_ge(sems[who], (n + 1 - who) // 2)

        def xparts(p, g):
            w = p.H * 2 * PARTS * p.K
            v = Xt[:, g * XG * w:(g + 1) * XG * w]
            return v.rearrange("p (m t k) -> p m t k", t=PARTS, k=p.K)

        def xf_view(p, g):
            v = xf[g % 2][:, 0:XG * p.H * 2 * p.K]
            return v.rearrange("p (m k) -> p m k", k=p.K)

        def pro_sync(p):
            if p.l == 0:
                sync.dma_start(ident[:, :], ident_in).then_inc(p.s["const_in"], 16)
                sync.dma_start(sel[:, :, :], sel_in).then_inc(p.s["const_in"], 16)
            src = xv if p.l == 0 else x1v
            for g in range(LG):
                sync.dma_start(x_all[:, g * LB:(g + 1) * LB, :], src[:, g * LB:(g + 1) * LB, :]).then_inc(p.x_in[g], 16)
            H, HD = p.H, p.HD
            mats = (W1, W2) if p.l == 0 else (Ww, Ww)
            biases = (b1, b2) if p.l == 0 else (Wb, Wb)
            for k in range(2):
                sync.dma_start(wn[k], mats[k]).then_inc(p.s["w_in"], 16)
                sync.dma_start(bcol[k], biases[k].rearrange("(p o) -> p o", o=1)).then_inc(p.s["w_in"], 16)
            sync.dma_start(wcat[:, 0:128], W3T if p.l == 0 else WwT).then_inc(p.s["w_in"], 16)
            sync.dma_start(brow[:, 0:128], (b3 if p.l == 0 else Wb).rearrange("(o n) -> o n", o=1)).then_inc(p.s["w_in"], 16)
            sync.wait_ge(p.s["consts"], 1)
            for k in range(2):
                for h in range(H):
                    row = (a[h, k * HD:(k + 1) * HD] if p.l == 0 else aw[0, k * HD:(k + 1) * HD])
                    sync.dma_start(ablk[k][h * HD:(h + 1) * HD, h:h + 1],
                                   row.rearrange("(p o) -> p o", o=1)).then_inc(p.s["w_in"], 16)
            if p.l == 1:
                sync.dma_start(abrow[0:1, 0:1], ab.rearrange("(o n) -> o n", o=1)).then_inc(p.s["w_in"], 16)
                for g in range(LG):
                    sync.wait_ge(p.s["h_done"], (g + 1) * LB)
                    sync.dma_start(h1v[:, g * LB:(g + 1) * LB, :],
                                   x_all[:, g * LB:(g + 1) * LB, :]).then_inc(p.s["h_stored"], 16)
            copied(sync, p.s["s1_copied"], p.n_s)
            sync.dma_start(s1_rows[p.l], s1_sb[0:H, :]).then_inc(p.s["s1_stored"], 16)
            sync.wait_ge(p.s["s1_stored"], 16)
            if p.l == 1:
                sync.wait_ge(p.s["h_stored"], 16 * LG)

        def n_weights(p):
            return 16 * (6 + 2 * p.H + (p.l == 1))

        def pro_pool(p):
            H, HD, K = p.H, p.HD, p.K
            if p.l == 0:
                pool.memset(ones[:, :], 1.0)
                pool.memset(minus1[:, :], -1.0)
                pool.memset(minus_half[:, :], -0.5)
            pool.memset(ablk[0], 0.0)
            pool.memset(ablk[1], 0.0)
            pool.memset(sumV[:, :], float(N)).then_inc(p.s["consts"], 1)
            pool.wait_ge(p.s["consts"], 1)
            for g in range(LG):
                pool.wait_ge(p.s["var_done"], g + 1)
                s = slice(g * LB, (g + 1) * LB)
                pool.tensor_tensor(stat[:, 1, s], stat[:, 1, s], minus_half[:, s], ALU.pow).then_inc(p.s["rstd_done"], 1)
            pool.wait_ge(p.s["local_max"], 1)
            pool.partition_all_reduce(Smax[:, 1, 0:H], Smax[:, 0, 0:H], P, bass.bass_isa.ReduceOp.max).then_inc(p.s["global_max"], 1)
            pool.wait_ge(p.s["b_exp"], 4)
            copied(pool, p.s["v_copied"], p.n_v)
            pool.wait_ge(p.s["s1_in_psum"], p.n_s)
            Vv, _, _ = p.views()
            for g in range(p.groups):
                if g >= 2:
                    pool.wait_ge(p.s["lo_done"], g - 1)
                o = xf_view(p, g).rearrange("p (b h t) k -> p b h t k", h=H, t=2)
                bl = slice(g * XG, (g + 1) * XG)
                for b in range(XG):
                    for t in range(2):
                        w = bexp[:, g * XG + b, 0:H, t]
                        pool.tensor_tensor(o[:, b, :, t, 0:HD], Vv[:, g * XG + b, :].rearrange("p (h d) -> p h d", h=H),
                                           bc(w, HD), ALU.mult)
                    last = pool.tensor_copy(o[:, b, :, :, HD], bexp[:, g * XG + b, 0:H, :])
                last.then_inc(p.s["xf_ready"], 1)

        def pro_dve(p):
            H, HD, K = p.H, p.HD, p.K
            steps = [0]

            def chain(ins):
                steps[0] += 1
                ins.then_inc(p.s["dve_step"], 1)
                dve.wait_ge(p.s["dve_step"], steps[0])

            for g in range(LG):
                s = slice(g * LB, (g + 1) * LB)
                xg = x_all[:, s, :]
                dve.wait_ge(p.x_in[g], 16)
                chain(nc.vector.reduce_sum(stat[:, 0, s], xg, axis=AX.X))
                chain(nc.vector.tensor_scalar(stat[:, 0, s], stat[:, 0, s], 1.0 / D, None, ALU.mult))
                nc.vector.tensor_tensor(xg, xg, bc(stat[:, 0, s], D), ALU.subtract).then_inc(p.s["centred"], 1)
                dve.wait_ge(p.s["squared"], g + 1)
                chain(nc.vector.reduce_sum(stat[:, 1, s], sq[:, s, :], axis=AX.X))
                nc.vector.tensor_scalar(stat[:, 1, s], stat[:, 1, s], 1.0 / D, EPS, ALU.mult, ALU.add).then_inc(p.s["var_done"], 1)
            for g in range(LG):
                dve.wait_ge(p.s["rstd_done"], g + 1)
                for b in range(g * LB, (g + 1) * LB):
                    nc.vector.tensor_scalar(x_all[:, b, :], x_all[:, b, :], stat[:, 1, b:b + 1], 0.0,
                                            ALU.mult, ALU.max).then_inc(p.s["h_done"], 1)
            pro_copies(p, 1)
            Vv, s2v, s1v = p.views()
            copied(dve, p.s["v_copied"], p.n_v)
            nc.vector.tensor_reduce(Smax[:, 0, 0:H], s2v.rearrange("p b h -> p h b"), axis=AX.X, op=ALU.max).then_inc(p.s["local_max"], 1)
            nc.vector.tensor_scalar(thr[:, :, 0:H], s2v, -1.0, None, ALU.mult)
            nc.vector.tensor_scalar(steep_s2[:, :, 0:H], s2v, STEEP, None, ALU.mult)
            dve.wait_ge(p.s["global_max"], 1)
            S = Smax[:, 1, 0:H].unsqueeze(1).to_broadcast([P, NB, H])
            nc.vector.tensor_tensor(mrow[:, :, 0:H], s2v, S, ALU.subtract).then_inc(p.s["shifted"], 1)
            chain(nc.vector.tensor_tensor(zrow[:, :, 0:H], s1v, S, ALU.add))
            chain(nc.vector.scalar_tensor_tensor(out=Ai[:, :, 0:H], in0=zrow[:, :, 0:H], scalar=SLOPE, in1=zrow[:, :, 0:H],
                                                 op0=ALU.mult, op1=ALU.max))
            nc.vector.scalar_tensor_tensor(out=Ci[:, :, 0:H], in0=zrow[:, :, 0:H], scalar=SLOPE, in1=Ai[:, :, 0:H],
                                           op0=ALU.mult, op1=ALU.subtract)
            chain(nc.vector.tensor_tensor(zrow[:, :, 0:H], zrow[:, :, 0:H], Ai[:, :, 0:H], ALU.subtract))
            nc.vector.tensor_copy(Ai[:, :, 0:H], zrow[:, :, 0:H]).then_inc(p.s["ac_ready"], 1)
            dve.wait_ge(p.s["sumv_in_psum"], 1)
            dve.wait_ge(p.s["consts"], 1)
            nc.vector.tensor_copy(sumV[:, 0:H * K].rearrange("p (h k) -> p h k", k=K)[:, :, 0:HD],
                                  bank[7][:, 0:128].rearrange("p (h d) -> p h d", d=HD))
            for g in range(p.groups):
                o, xs = xf_view(p, g), xparts(p, g)
                dve.wait_ge(p.s["hi_done"], g + 1)
                nc.vector.tensor_tensor(o, o, xs[:, :, 0, :], ALU.subtract).then_inc(p.s["rest1"], 1)
                dve.wait_ge(p.s["mid_done"], g + 1)
                nc.vector.tensor_tensor(xs[:, :, 2, :], o, xs[:, :, 1, :], ALU.subtract).then_inc(p.s["lo_done"], 1)

        def pro_copies(p, who):
            def copy(o, i):
                return nc.scalar.copy(o, i) if who == 0 else nc.vector.tensor_copy(o, i)
            eng = act if who == 0 else dve
            for t in range(p.n_t):
                if t % 2 == who:
                    eng.wait_ge(p.s["hT_in_psum"], t + 1)
                    copy(hT[:, t * 512:(t + 1) * 512], bank[t % 4][:, :]).then_inc(p.s["hT_copied"][who], 1)
            if who == 0:
                eng.wait_ge(p.s["u_in_psum"], 1)
                copy(wcat[:, 128:p.VW], bank[4][:, 0:2 * p.H]).then_inc(p.s["u_copied"], 1)
                eng.wait_ge(p.s["b_in_psum"], 1)
                copy(brow[:, 128:p.VW], bank[5][0:1, 0:2 * p.H]).then_inc(p.s["b_copied"], 1)
            for t in range(p.n_v):
                if t % 2 == who:
                    eng.wait_ge(p.s["v_in_psum"], t + 1)
                    copy(V32[:, 2 * t:2 * t + 2, 0:p.VW],
                         bank[t % 4][:, 0:2 * p.VW].rearrange("p (b n) -> p b n", b=2)).then_inc(p.s["v_copied"][who], 1)
            for t in range(p.n_s):
                if t % 2 == who:
                    eng.wait_ge(p.s["s1_in_psum"], t + 1)
                    copy(s1_sb[0:p.H, t * 512:(t + 1) * 512], bank[4 + t % 2][0:p.H, :]).then_inc(p.s["s1_copied"][who], 1)

        def pro_act(p):
            H, HD, K = p.H, p.HD, p.K
            for g in range(LG):
                s = slice(g * LB, (g + 1) * LB)
                act.wait_ge(p.s["centred"], g + 1)
                nc.scalar.activation(sq[:, s, :], x_all[:, s, :], ACT.Square).then_inc(p.s["squared"], 1)
            pro_copies(p, 0)
            act.wait_ge(p.s["shifted"], 1)
            for e in range(2):
                for t in range(2):
                    power = (t + e * p.l) % 2
                    nc.scalar.activation(bexp[:, :, e:H:2, t], mrow[:, :, e:H:2], ACT.Exp,
                                         scale=SLOPE if power else 1.0).then_inc(p.s["b_exp"], 1)
            act.wait_ge(p.s["ac_ready"], 1)
            nc.scalar.activation(Ai[:, :, 0:H], Ai[:, :, 0:H], ACT.Exp)
            nc.scalar.activation(Ci[:, :, 0:H], Ci[:, :, 0:H], ACT.Exp).then_inc(p.s["ac_exp"], 1)
            act.wait_ge(p.s["s1_stored"], 16)
            for g in range(p.groups):
                o, xs = xf_view(p, g), xparts(p, g)
                act.wait_ge(p.s["xf_ready"], g + 1)
                nc.scalar.copy(xs[:, :, 0, :], o).then_inc(p.s["hi_done"], 1)
                act.wait_ge(p.s["rest1"], g + 1)
                nc.scalar.copy(xs[:, :, 1, :], o).then_inc(p.s["mid_done"], 1)

        def pro_pe(p):
            H, HD, K = p.H, p.HD, p.K
            pe.wait_ge(pro[0].s["const_in"], 32)
            pe.wait_ge(pro[0].s["consts"], 1)
            pe.wait_ge(p.s["w_in"], n_weights(p))
            for k, o in ((1, 0), (0, H)):
                last = nc.tensor.matmul(bank[4][:, o:o + H], wn[k], ablk[k][:, 0:H], start=True, stop=True)
            last.then_inc(p.s["u_in_psum"], 1)
            nc.tensor.matmul(bank[5][0:1, 0:H], bcol[1], ablk[1][:, 0:H], start=True, stop=True)
            last = nc.tensor.matmul(bank[5][0:1, H:2 * H], bcol[0], ablk[0][:, 0:H], start=True, stop=p.l == 0)
            if p.l == 1:
                last = nc.tensor.matmul(bank[5][0:1, H:2 * H], ones[0:1, 0:1], abrow[0:1, 0:1].to_broadcast([1, H]), start=False, stop=True)
            last.then_inc(p.s["b_in_psum"], 1)
            for t in range(p.n_t):
                pe.wait_ge(p.s["h_done"], 4 * t + 4)
                if t >= 4:
                    copied(pe, p.s["hT_copied"], t - 3)
                for b in range(4):
                    last = nc.tensor.transpose(bank[t % 4][:, b * P:(b + 1) * P], x_all[:, 4 * t + b, :], ident[:, :])
                last.then_inc(p.s["hT_in_psum"], 1)
            copied(pe, p.s["hT_copied"], p.n_t)
            pe.wait_ge(p.s["u_copied"], 1)
            pe.wait_ge(p.s["b_copied"], 1)
            if p.l == 1:
                pe.wait_ge(p.s["h_stored"], 16 * LG)
            for t in range(p.n_v):
                if t >= 4:
                    copied(pe, p.s["v_copied"], t - 3)
                for b in range(2):
                    o = bank[t % 4][:, b * p.VW:(b + 1) * p.VW]
                    nc.tensor.matmul(o, ones[0:1, 0:P], brow[0:1, 0:p.VW], start=True, stop=False)
                    last = nc.tensor.matmul(o, hT[:, (2 * t + b) * P:(2 * t + b + 1) * P], wcat[:, 0:p.VW],
                                            start=False, stop=True)
                last.then_inc(p.s["v_in_psum"], 1)
            for t in range(p.n_s):
                if t >= 2:
                    copied(pe, p.s["s1_copied"], t - 1)
                o = bank[4 + t % 2][0:H, :]
                nc.tensor.matmul(o, brow[0:1, 128 + H:p.VW], ones[0:1, :], start=True, stop=False)
                nc.tensor.matmul(o, wcat[:, 128 + H:p.VW], hT[:, t * 512:(t + 1) * 512],
                                 start=False, stop=True).then_inc(p.s["s1_in_psum"], 1)
            copied(pe, p.s["v_copied"], p.n_v)
            for b in range(NB):
                last = nc.tensor.matmul(bank[7][:, 0:128], ones[:, 0:P], V32[:, b, 0:128], start=b == 0, stop=b == NB - 1)
            last.then_inc(p.s["sumv_in_psum"], 1)

        pro = [Prologue(0), Prologue(1)]

        adj_v = adj.rearrange("(c i p) (q j) -> c q p i j", i=IB, p=P, j=JP * P)
        xchunk = x.rearrange("(c i p) d -> c p i d", i=IB, p=P)
        x1chunk = x1_dram.rearrange("(c i p) d -> c p i d", i=IB, p=P)
        s1row0 = s1_rows[0].rearrange("h (c n) -> c h n", n=CH)
        nat_in = [sem(f"nat_in{s}") for s in range(SLOTS)]
        transposed = [sem(f"transposed{s}") for s in range(SLOTS)]
        shrunk = [sem(f"shrunk{s}") for s in range(SLOTS)]
        mask_stored = [sem(f"mask_stored{s}") for s in range(2)]
        s1bc_in = sem("s1bc_in")
        side_ready0 = sem("side_ready0")
        plus_ready0 = sem("plus_ready0")
        minus_ready0 = sem("minus_ready0")
        masks_free0 = sem("masks_free0")
        sums_ready0 = sem("sums_ready0")
        bank_free0 = [sem("bank_free0_act"), sem("bank_free0_dve")]
        stage_free0 = sem("stage_free0")
        x_chunk_in = sem("x_chunk_in")
        x1_ready = sem("x1_ready")
        x1_stored = sem("x1_stored")
        pool_step0 = sem("pool_step0")
        X0 = Xt[:, 0:NB * H0 * 2 * PARTS * K0].rearrange("p (b h t k) -> p b h t k", h=H0, t=2, k=PARTS * K0)

        def at(c, per, k):
            return c * per + k

        def side0(c, k):
            act.wait_ge(masks_free0, at(c, NG0, k + 1))
            for h in range(H0):
                for j in range(GJ0):
                    last = nc.scalar.activation(mplus[k % SLOTS][h][:, j, :], s1bc0[:, h, :], ACT.Sigmoid, scale=STEEP,
                                                bias=steep_s2[:, k * GJ0 + j, h:h + 1])
                last.then_inc(side_ready0, 1)

        def s1_load0(c):
            act.dma_start(s1bc0, s1row0[c].unsqueeze(0).to_broadcast([P, H0, CH])).then_inc(s1bc_in, 16)

        def copy_out0(c, who):
            eng, copy = (act, nc.scalar.copy) if who == 0 else (dve, nc.vector.tensor_copy)
            eng.wait_ge(stage_free0, at(c, IB, IB))
            for n in range(4):
                i, h = 2 * who + n // 2, n % 2
                eng.wait_ge(sums_ready0, at(c, 8, 4 * who + n + 1))
                copy(stage0[:, i, h, :], bank[4 * who + n][:, 0:2 * PARTS * K0]).then_inc(bank_free0[who], 1)

        def main0_act():
            act.sem_inc(bank_free0[0], 4)
            s1_load0(0)
            act.wait_ge(s1bc_in, 16)
            for k in range(AHEAD):
                side0(0, k)

            def chunk(c, more):
                for k in range(AHEAD, NG0):
                    side0(c, k)
                if more:
                    act.wait_ge(side_ready0, at(c, 2 * NG0, 2 * NG0))
                    s1_load0(c + 1)
                    act.wait_ge(s1bc_in, at(c, 16, 32))
                    for k in range(AHEAD):
                        side0(c + 1, k)
                copy_out0(c, 0)

            with act.Fori(0, NCH - 1) as c:
                chunk(c, True)
            chunk(NCH - 1, False)

        def masks0(c, k):
            q, half = k * GJ0 // JP, k * GJ0 % JP
            if half == 0:
                dve.wait_ge(transposed[q % SLOTS], at(c, 64 * NP0 // SLOTS, 64 * (q // SLOTS + 1)))
            m0 = adjT[q % SLOTS][:, half:half + GJ0, :]
            for h in range(H0):
                dve.wait_ge(side_ready0, at(c, 2 * NG0, 2 * k + h + 1))
                m = mplus[k % SLOTS][h]
                nc.vector.tensor_tensor(m, m, m0, ALU.mult).then_inc(plus_ready0, 1)
            for h in range(H0):
                dve.wait_ge(plus_ready0, at(c, 2 * NG0, 2 * k + h + 1))
                nc.vector.tensor_tensor(mminus[k % SLOTS][h], m0, mplus[k % SLOTS][h], ALU.subtract).then_inc(minus_ready0, 1)

        def main0_dve():
            dve.sem_inc(bank_free0[1], 4)
            for k in range(AHEAD):
                masks0(0, k)

            def chunk(c, more):
                for k in range(AHEAD, NG0):
                    masks0(c, k)
                if more:
                    for k in range(AHEAD):
                        masks0(c + 1, k)
                copy_out0(c, 1)

            with dve.Fori(0, NCH - 1) as c:
                chunk(c, True)
            chunk(NCH - 1, False)

        def main0_pe():
            pe.sem_inc(masks_free0, SLOTS)
            with pe.Fori(0, NCH) as c:
                for k in range(NG0):
                    pe.wait_ge(plus_ready0, at(c, 2 * NG0, 2 * k + 2))
                    pe.wait_ge(minus_ready0, at(c, 2 * NG0, 2 * k + 2))
                    for j in range(GJ0):
                        b = k * GJ0 + j
                        for i in range(IB):
                            for h in range(H0):
                                n = 2 * i + h
                                if b == 0:
                                    pe.wait_ge(bank_free0[n // 4], at(c, 4, n % 4 + 1))
                                for t, m in enumerate((mplus, mminus)):
                                    last = nc.tensor.matmul(
                                        bank[n][:, t * PARTS * K0:(t + 1) * PARTS * K0],
                                        m[k % SLOTS][h][:, j, i * P:(i + 1) * P], X0[:, b, h, t, :],
                                        start=b == 0 and t == 0, stop=b == NB - 1 and t == 1, skip_group_check=True)
                                if b == NB - 1:
                                    last.then_inc(sums_ready0, 1)
                    if k < NG0 - 1:
                        last.then_inc(masks_free0, 1)
                    else:
                        pe.wait_ge(sums_ready0, at(c, 8, 8))
                        pe.sem_inc(masks_free0, 1)

        def main0_sync():
            def piece(c, q, first):
                s = q % SLOTS
                wait_alone(sync, nat_in[s], at(c, 16 * NP0 // SLOTS, 16 * (q // SLOTS + 1)))
                if not (first and q < SLOTS):
                    wait_alone(sync, minus_ready0, at(c, 2 * NG0, 2 * (q - SLOTS + 1) * JP // GJ0))
                    wait_alone(sync, shrunk[s], at(c, 16 * NP0 // SLOTS, 16 * (q // SLOTS)))
                for i in range(IB):
                    sync.dma_start_transpose(adjT[s][:, :, i * P:(i + 1) * P], nat[s][:, i, :]).then_inc(transposed[s], 16)

            def store(c, q):
                wait_alone(sync, shrunk[q % SLOTS], at(c, 16 * NP0 // SLOTS, 16 * (q // SLOTS + 1)))
                sync.dma_start(adjT8[c, q], small[q % 2].rearrange("p j n -> p (j n)").bitcast(u8)).then_inc(mask_stored[q % 2], 16)

            for q in range(NP0):
                piece(0, q, True)
                if q >= 2:
                    store(0, q - 2)
            with sync.Fori(1, NCH) as c:
                for q in range(NP0):
                    piece(c, q, False)
                    if q < 2:
                        store(c - 1, NP0 + q - 2)
                    else:
                        store(c, q - 2)
            for q in (NP0 - 2, NP0 - 1):
                store(NCH - 1, q)
            for s in range(2):
                sync.wait_ge(mask_stored[s], 16 * NCH * NP0 // 2)

        def main0_pool():
            steps = [0]
            EPS_PER = 9

            def load(c, q, first):
                s = q % SLOTS
                if not (first and q < SLOTS):
                    wait_alone(pool, transposed[s], at(c, 64 * NP0 // SLOTS, 64 * (q // SLOTS)))
                pool.dma_start(nat[s], adj_v[c, q]).then_inc(nat_in[s], 16)

            def shrink(c, q, first):
                s = q % SLOTS
                wait_alone(pool, transposed[s], at(c, 64 * NP0 // SLOTS, 64 * (q // SLOTS + 1)))
                if not (first and q < 2):
                    wait_alone(pool, mask_stored[q % 2], at(c, 16 * NP0 // 2, 16 * (q // 2)))
                pool.dma_start(small[q % 2], adjT[s]).then_inc(shrunk[s], 16)

            def norm(c, i):
                n = [0]

                def chain(ins):
                    n[0] += 1
                    ins.then_inc(pool_step0, 1)
                    wait_alone(pool, pool_step0, at(c, 10 * IB, 10 * i + n[0]))

                if i == 0:
                    pool.dma_start(x_in[:, :, :], xchunk[c]).then_inc(x_chunk_in, 16)
                for who in range(2):
                    if i == 2 * who:
                        wait_alone(pool, bank_free0[who], at(c, 4, 8))
                bi = c * IB + i
                st = stage0[:, i, :, :].rearrange("p h (t k) -> p h t k", t=2)
                plus, minus = st[:, :, 0, :], st[:, :, 1, :]
                A = bc(Ai[:, bass.ds(bi, 1), 0:H0].rearrange("p o h -> p (o h)"), PARTS * K0)
                C = bc(Ci[:, bass.ds(bi, 1), 0:H0].rearrange("p o h -> p (o h)"), PARTS * K0)
                pool.tensor_tensor(plus, plus, A, ALU.mult)
                chain(pool.tensor_tensor(minus, minus, C, ALU.mult))
                chain(pool.tensor_tensor(w0[:, :, :], plus, minus, ALU.add))
                pool.sem_inc(stage_free0, 1)
                chain(pool.tensor_tensor(w0[:, :, 0:K0], w0[:, :, 0:K0], w0[:, :, K0:2 * K0], ALU.add))
                chain(pool.tensor_tensor(w0[:, :, 0:K0], w0[:, :, 0:K0], w0[:, :, 2 * K0:3 * K0], ALU.add))
                chain(pool.tensor_scalar(flag0[:, :], w0[:, :, HD0], 0.0, None, ALU.is_equal))
                chain(pool.tensor_tensor(w0[:, :, K0:2 * K0], sumV[:, 0:H0 * K0].rearrange("p (h k) -> p h k", k=K0),
                                         bc(flag0[:, :], K0), ALU.mult))
                chain(pool.tensor_tensor(w0[:, :, 0:K0], w0[:, :, 0:K0], w0[:, :, K0:2 * K0], ALU.add))
                chain(pool.tensor_tensor(rec0[:, :], w0[:, :, HD0], minus1[:, 0:H0], ALU.pow))
                chain(pool.tensor_tensor(w0[:, :, 0:HD0], w0[:, :, 0:HD0], bc(rec0[:, :], HD0), ALU.mult))
                if i == 0:
                    wait_alone(pool, x_chunk_in, at(c, 16, 16))
                chain(pool.tensor_tensor(x1_sb[:, i, :].rearrange("p (h d) -> p h d", h=H0),
                                         x_in[:, i, :].rearrange("p (h d) -> p h d", h=H0), w0[:, :, 0:HD0], ALU.add))
                if i == IB - 1:
                    pool.dma_start(x1chunk[c], x1_sb[:, :, :]).then_inc(x1_stored, 16)
                    wait_alone(pool, x1_stored, at(c, 16, 16))

            when = {NP0 * (2 * i + 2) // 10: i for i in range(IB)}
            if NP0 < 10:
                when = {}

            def chunk(c, first):
                for q in range(NP0):
                    load(c, q, first)
                    if q >= 2:
                        shrink(c, q - 2, first)
                    elif not first:
                        shrink(c - 1, NP0 + q - 2, False)
                    if not first and q in when:
                        norm(c - 1, when[q])
                if not first and not when:
                    for i in range(IB):
                        norm(c - 1, i)

            pool.sem_inc(stage_free0, IB)
            chunk(0, True)
            with pool.Fori(1, NCH) as c:
                chunk(c, False)
            for q in (NP0 - 2, NP0 - 1):
                shrink(NCH - 1, q, False)
            for i in range(IB):
                norm(NCH - 1, i)
            pool.wait_ge(x1_stored, 16 * NCH)

        adj8_v = adjT8.rearrange("c (q r) p n -> c q p r n", r=JQ // JP)
        s1row1 = s1_rows[1].rearrange("h (c n) -> c h n", n=CH)
        aggchunk = agg_dram.rearrange("(c i p) (h d) -> c p i h d", i=IB, p=P, d=HD1)
        X1 = Xt[:, 0:NB * H1 * 2 * PARTS * K1].rearrange("p (b k) -> p b k", b=NB)
        M1 = 2 * PARTS * K1
        PER_GROUP = JQ // GJ1

        class Sweep:
            s = {}

            def __init__(self, w):
                self.w, self.heads = w, [HS * w + n for n in range(HS)]
                self.c0, self.c1 = w * NCH, (w + 1) * NCH

            @classmethod
            def name_semaphores(cls):
                for name in ("s1A_in", "s1D_in", "side_act", "side_dve", "mask_ready", "masks_free", "sums_ready",
                             "bank_free_act", "bank_free_dve", "stage_free", "comb_in_psum",
                             "comb_copied", "comb_free", "step", "agg_stored"):
                    cls.s[name] = sem(f"l1_{name}")
                cls.adj_in = [sem(f"l1_adj_in{s}") for s in range(SLOTS)]

        Sweep.name_semaphores()

        ORDER = ((0, 1, 4), (2, 3, 5))

        def s1_load(w, c, who):
            eng, dst, done = ((act, s1bcA, w.s["s1A_in"]), (sync, s1bcD, w.s["s1D_in"]))[who]
            h = w.heads[2 * who]
            eng.dma_start(dst, s1row1[c - w.c0, h:h + 2].unsqueeze(0).to_broadcast([P, 2, CH])).then_inc(done, 16)

        def side1_act(w, c, k):
            wait_alone(act, w.s["masks_free"], at(c, NG1, k + 1))
            for n in range(2):
                for j in range(GJ1):
                    last = nc.scalar.activation(mask8[k % SLOTS][n][:, j, :], s1bcA[:, n, :], ACT.Sigmoid, scale=STEEP,
                                                bias=steep_s2[:, k * GJ1 + j, w.heads[n]:w.heads[n] + 1], saturate=False)
                last.then_inc(w.s["side_act"], 1)

        def copy_out1(w, c, who):
            eng, copy = (act, nc.scalar.copy) if who == 0 else (dve, nc.vector.tensor_copy)
            free = w.s["bank_free_act"] if who == 0 else w.s["bank_free_dve"]
            wait_alone(eng, w.s["stage_free"], at(c, 1, 1))
            for n, b in enumerate(ORDER[who]):
                wait_alone(eng, w.s["sums_ready"], at(c, 6, b + 1))
                copy(stage1[0:M1, b, :], bank[b][0:M1, :]).then_inc(free, 1)

        def comb_out(w, c):
            wait_alone(act, w.s["comb_free"], at(c, 1, 1))
            wait_alone(act, w.s["comb_in_psum"], at(c, 1, 1))
            for i2 in range(2):
                nc.scalar.copy(comb[:, 2 * i2:2 * i2 + 2, :, :].rearrange("p i h k -> p (i h k)"),
                               bank[6 + i2][:, 0:2 * HS * 2 * K1]).then_inc(w.s["comb_copied"], 1)

        def main1_act(w):
            if w.w == 0:
                act.sem_inc(w.s["bank_free_act"], 3)
                act.sem_inc(w.s["comb_copied"], 2)
            s1_load(w, w.c0, 0)
            act.wait_ge(w.s["s1A_in"], at(w.c0, 16, 16))
            for k in range(LATE):
                side1_act(w, w.c0, k)

            def chunk(c, more):
                for k in range(LATE, NG1):
                    side1_act(w, c, k)
                if more:
                    wait_alone(act, w.s["side_act"], at(c, 2 * NG1, 2 * NG1))
                    s1_load(w, c + 1, 0)
                    wait_alone(act, w.s["s1A_in"], at(c, 16, 32))
                    for k in range(AHEAD):
                        side1_act(w, c + 1, k)
                copy_out1(w, c, 0)
                if more:
                    for k in range(AHEAD, LATE):
                        side1_act(w, c + 1, k)
                comb_out(w, c)

            with act.Fori(w.c0, w.c1 - 1) as c:
                chunk(c, True)
            chunk(w.c1 - 1, False)

        def masks1(w, c, k):
            wait_alone(dve, w.s["masks_free"], at(c, NG1, k + 1))
            for n in range(2, 4):
                for j in range(GJ1):
                    last = nc.vector.tensor_scalar(mask8[k % SLOTS][n][:, j, :], s1bcD[:, n - 2, :],
                                                   thr[:, k * GJ1 + j, w.heads[n]:w.heads[n] + 1], None, ALU.is_ge, saturate=False)
                last.then_inc(w.s["side_dve"], 1)
            q, part = k // PER_GROUP, k % PER_GROUP
            if part == 0:
                wait_alone(dve, w.adj_in[q % SLOTS], at(c, 16 * NP1 // SLOTS, 16 * (q // SLOTS + 1)))
            m0 = adj8[q % SLOTS][:, part * GJ1:(part + 1) * GJ1, :].rearrange("p j n -> p (j n)").bitcast(i32)
            for n in range(HS):
                if n < 2:
                    wait_alone(dve, w.s["side_act"], at(c, 2 * NG1, 2 * k + n + 1))
                else:
                    wait_alone(dve, w.s["side_dve"], at(c, 2 * NG1, 2 * k + n - 1))
                m = mask8[k % SLOTS][n].rearrange("p j n -> p (j n)").bitcast(i32)
                nc.vector.tensor_tensor(m, m, m0, ALU.bitwise_and).then_inc(w.s["mask_ready"], 1)

        def main1_dve(w):
            if w.w == 0:
                dve.sem_inc(w.s["bank_free_dve"], 3)
            dve.wait_ge(w.s["s1D_in"], at(w.c0, 16, 16))
            for k in range(AHEAD):
                masks1(w, w.c0, k)

            def chunk(c, more):
                for k in range(AHEAD, NG1):
                    masks1(w, c, k)
                if more:
                    wait_alone(dve, w.s["s1D_in"], at(c, 16, 32))
                    for k in range(AHEAD):
                        masks1(w, c + 1, k)
                copy_out1(w, c, 1)

            with dve.Fori(w.c0, w.c1 - 1) as c:
                chunk(c, True)
            chunk(w.c1 - 1, False)

        def main1_pe(w):
            if w.w == 0:
                pe.sem_inc(w.s["masks_free"], SLOTS)
            if w.w == 0:
                pe.sem_inc(w.s["stage_free"], 1)

            def group(c, k):
                wait_alone(pe, w.s["mask_ready"], at(c, HS * NG1, HS * (k + 1)))
                q, part = k // PER_GROUP, k % PER_GROUP
                for j in range(GJ1):
                    b = k * GJ1 + j
                    for n in range(6):
                        if b == 0:
                            who = 0 if n in ORDER[0] else 1
                            wait_alone(pe, (w.s["bank_free_act"], w.s["bank_free_dve"])[who], at(c, 3, ORDER[who].index(n) + 1))
                        if n < HS:
                            lhsT, rhs = X1[:, b, w.heads[n] * M1:(w.heads[n] + 1) * M1], mask8[k % SLOTS][n][:, j, :]
                        else:
                            o = w.heads[2 * (n - HS)] * M1 + M1 // 2
                            lhsT, rhs = X1[:, b, o:o + M1], adj8[q % SLOTS][:, part * GJ1 + j, :]
                        last = nc.tensor.matmul(bank[n][0:M1, :], lhsT, rhs, start=b == 0, stop=b == NB - 1)
                        if b == NB - 1:
                            last.then_inc(w.s["sums_ready"], 1)
                if k < NG1 - 1:
                    last.then_inc(w.s["masks_free"], 1)
                else:
                    wait_alone(pe, w.s["sums_ready"], at(c, 6, 6))
                    pe.sem_inc(w.s["masks_free"], 1)

            def combine(c):
                wait_alone(pe, w.s["bank_free_act"], at(c, 3, 6))
                wait_alone(pe, w.s["bank_free_dve"], at(c, 3, 6))
                wait_alone(pe, w.s["comb_copied"], at(c, 2, 2))
                for i in range(IB):
                    for n in range(HS):
                        o = bank[6 + i // 2][:, (i % 2) * HS * 2 * K1 + n * 2 * K1:(i % 2) * HS * 2 * K1 + (n + 1) * 2 * K1]
                        nc.tensor.matmul(o, stage1[0:M1, n, i * P:(i + 1) * P], sel[0:M1, n % 2, :], start=True, stop=False)
                        last = nc.tensor.matmul(o, stage1[0:M1, HS + n // 2, i * P:(i + 1) * P], sel[0:M1, 2 + n % 2, :],
                                                start=False, stop=True)
                last.then_inc(w.s["comb_in_psum"], 1)
                wait_alone(pe, w.s["comb_in_psum"], at(c, 1, 1))
                pe.sem_inc(w.s["stage_free"], 1)

            for k in range(AHEAD):
                group(w.c0, k)

            def chunk(c, more):
                for k in range(AHEAD, NG1):
                    group(c, k)
                if more:
                    for k in range(AHEAD):
                        group(c + 1, k)
                combine(c)

            with pe.Fori(w.c0, w.c1 - 1) as c:
                chunk(c, True)
            chunk(w.c1 - 1, False)

        def main1_sync(w):
            def piece(c, q, first):
                s = q % SLOTS
                if not (first and q < SLOTS):
                    wait_alone(sync, w.s["masks_free"], at(c, NG1, (q - SLOTS + 1) * PER_GROUP + SLOTS))
                sync.dma_start(adj8[s].rearrange("p (r j) n -> p r (j n)", r=JQ // JP).bitcast(u8), adj8_v[c - w.c0, q]).then_inc(w.adj_in[s], 16)

            def chunk(c, first):
                for q in range(NP1):
                    piece(c, q, first)
                    if q == min(1, NP1 - 1) and not first:
                        wait_alone(sync, w.s["side_dve"], at(c, 2 * NG1, 0))
                        s1_load(w, c, 1)

            s1_load(w, w.c0, 1)
            chunk(w.c0, True)
            with sync.Fori(w.c0 + 1, w.c1) as c:
                chunk(c, False)

        def main1_pool(w):
            if w.w == 0:
                pool.sem_inc(w.s["comb_free"], 1)
            with pool.Fori(w.c0, w.c1) as c:
                n = [0]

                def chain(ins):
                    n[0] += 1
                    ins.then_inc(w.s["step"], 1)
                    wait_alone(pool, w.s["step"], at(c, 8, n[0]))

                wait_alone(pool, w.s["comb_copied"], at(c, 2, 4))
                for t, (src, dst) in enumerate(((Ai, ep), (Ci, ep2))):
                    for i in range(IB):
                        v = src[:, bass.ds((c - w.c0) * IB + i, 1), w.heads[0]:w.heads[0] + HS].rearrange("p o h -> p (o h)")
                        last = pool.tensor_tensor(dst[:, i * HS:(i + 1) * HS, :], comb[:, i, :, t * K1:(t + 1) * K1],
                                                  bc(v, K1), ALU.mult)
                    chain(last)
                pool.sem_inc(w.s["comb_free"], 1)
                chain(pool.tensor_tensor(ep[:, :, :], ep[:, :, :], ep2[:, :, :], ALU.add))
                chain(pool.tensor_scalar(flag1, ep[:, :, HD1], 0.0, None, ALU.is_equal))
                s = sumV[:, w.heads[0] * K1:(w.heads[0] + HS) * K1].rearrange("p (h k) -> p h k", k=K1)
                for i in range(IB):
                    last = pool.tensor_tensor(ep2[:, i * HS:(i + 1) * HS, :], s, bc(flag1[:, i * HS:(i + 1) * HS], K1), ALU.mult)
                chain(last)
                chain(pool.tensor_tensor(ep, ep, ep2, ALU.add))
                chain(pool.tensor_tensor(rec1, ep[:, :, HD1], minus1[:, 0:IB * HS], ALU.pow))
                chain(pool.tensor_tensor(agg_sb, ep[:, :, 0:HD1], bc(rec1, HD1), ALU.mult))
                pool.dma_start(aggchunk[c - w.c0][:, :, w.heads[0]:w.heads[0] + HS, :].rearrange("p i h d -> p i (h d)"),
                               agg_sb.rearrange("p (i h) d -> p i (h d)", i=IB)).then_inc(w.s["agg_stored"], 16)
                wait_alone(pool, w.s["agg_stored"], at(c, 16, 16))
            pool.wait_ge(w.s["agg_stored"], at(w.c1, 16, 0))

        sweeps = [Sweep(w) for w in range(H1 // HS)]

        aggv = agg_dram.rearrange("(b p) d -> p b d", p=P)
        outv = out.rearrange("(b p) d -> p b d", p=P)
        fin_in = [sem(f"fin_in{s}") for s in range(2)]
        fin_low = sem("fin_low")
        fin_exp = sem("fin_exp")
        fin_done = sem("fin_done")
        fin_sum = sem("fin_sum")
        fin_two = sem("fin_two")
        out_stored = [sem(f"out_stored{s}") for s in range(2)]

        def fin_sync():
            def store(t):
                sync.wait_ge(fin_done, t + 1)
                sync.dma_start(outv[:, t * FB:(t + 1) * FB, :], fin_e[t % 2]).then_inc(out_stored[t % 2], 16)

            for t in range(NF):
                if t >= 2:
                    sync.wait_ge(fin_done, t - 1)
                for dst, src in ((fin_y, aggv), (fin_h, h1v), (fin_x, x1v)):
                    sync.dma_start(dst[t % 2], src[:, t * FB:(t + 1) * FB, :]).then_inc(fin_in[t % 2], 16)
                if t >= 1:
                    store(t - 1)
            store(NF - 1)
            for s in range(2):
                sync.wait_ge(out_stored[s], 16 * NF // 2)

        def fin_dve():
            for t in range(NF):
                s = t % 2
                dve.wait_ge(fin_in[s], 48 * (t // 2 + 1))
                nc.vector.tensor_tensor(fin_y[s], fin_y[s], fin_h[s], ALU.add).then_inc(fin_sum, 1)
                if t >= 2:
                    dve.wait_ge(out_stored[s], 16 * (t // 2))
                dve.wait_ge(fin_sum, t + 1)
                nc.vector.tensor_scalar(fin_h[s], fin_y[s], 0.0, None, ALU.min).then_inc(fin_low, 1)
                dve.wait_ge(fin_exp, t + 1)
                nc.vector.scalar_tensor_tensor(out=fin_y[s], in0=fin_y[s], scalar=0.0, in1=fin_e[s],
                                               op0=ALU.max, op1=ALU.add).then_inc(fin_two, 1)
                dve.wait_ge(fin_two, t + 1)
                nc.vector.scalar_tensor_tensor(out=fin_e[s], in0=fin_y[s], scalar=-1.0, in1=fin_x[s],
                                               op0=ALU.add, op1=ALU.add).then_inc(fin_done, 1)

        def fin_act():
            for t in range(NF):
                act.wait_ge(fin_low, t + 1)
                nc.scalar.activation(fin_e[t % 2], fin_h[t % 2], ACT.Exp).then_inc(fin_exp, 1)

        @block.sync
        def _(eng):
            pro_sync(pro[0])
            phase_over(eng, 1)
            main0_sync()
            phase_over(eng, 2)
            pro_sync(pro[1])
            phase_over(eng, 3)
            for n, w in enumerate(sweeps):
                main1_sync(w)
                phase_over(eng, 4 + n)
            fin_sync()

        @block.scalar
        def _(eng):
            pro_act(pro[0])
            phase_over(eng, 1)
            main0_act()
            phase_over(eng, 2)
            pro_act(pro[1])
            phase_over(eng, 3)
            for n, w in enumerate(sweeps):
                main1_act(w)
                phase_over(eng, 4 + n)
            fin_act()

        @block.vector
        def _(eng):
            pro_dve(pro[0])
            phase_over(eng, 1)
            main0_dve()
            phase_over(eng, 2)
            pro_dve(pro[1])
            phase_over(eng, 3)
            for n, w in enumerate(sweeps):
                main1_dve(w)
                phase_over(eng, 4 + n)
            fin_dve()

        @block.tensor
        def _(eng):
            pro_pe(pro[0])
            phase_over(eng, 1)
            main0_pe()
            phase_over(eng, 2)
            pro_pe(pro[1])
            phase_over(eng, 3)
            for n, w in enumerate(sweeps):
                main1_pe(w)
                phase_over(eng, 4 + n)

        @block.gpsimd
        def _(eng):
            pro_pool(pro[0])
            phase_over(eng, 1)
            main0_pool()
            phase_over(eng, 2)
            pro_pool(pro[1])
            phase_over(eng, 3)
            for n, w in enumerate(sweeps):
                main1_pool(w)
                phase_over(eng, 4 + n)


def kernel(**inputs):
    import numpy as np
    import concourse.bacc as bacc
    from concourse import mybir
    from concourse.bass_utils import run_bass_kernel_spmd as run

    i = {k: np.ascontiguousarray(v) for k, v in inputs.items()}
    sel = np.zeros((128, 4, 2 * K1), np.float32)
    for part in range(PARTS):
        for k in range(K1):
            for e in range(2):
                sel[(e * PARTS + part) * K1 + k, e, k] = 1.0
                sel[((1 - e) * PARTS + part) * K1 + k, e, K1 + k] = -1.0
                sel[(e * PARTS + part) * K1 + k, 2 + e, K1 + k] = 1.0
    arrays = {
        "x": i["x"], "adj": i["adj"],
        "W1": i["L0_gnn_W1"], "b1": i["L0_gnn_b1"], "W2": i["L0_gnn_W2"], "b2": i["L0_gnn_b2"],
        "W3": i["L0_gnn_W3"], "W3T": np.ascontiguousarray(i["L0_gnn_W3"].T), "b3": i["L0_gnn_b3"], "a": i["L0_gnn_a"],
        "Ww": i["L1_gnn_W_w"], "WwT": np.ascontiguousarray(i["L1_gnn_W_w"].T), "Wb": i["L1_gnn_W_b"],
        "aw": i["L1_gnn_a_w"], "ab": i["L1_gnn_a_b"],
        "ident": np.eye(128, dtype=np.float32), "sel": sel,
    }
    nc = bacc.Bacc("TRN2", target_bir_lowering=False, num_devices=1)
    args = [nc.dram_tensor(f"in_{n}", v.shape, mybir.dt.from_np(v.dtype), kind="ExternalInput").ap()
            for n, v in arrays.items()]
    out = nc.dram_tensor("out_0", i["x"].shape, mybir.dt.float32, kind="ExternalOutput").ap()
    gat_kernel(nc, *args, out)
    r = run(nc, [{f"in_{n}": v for n, v in arrays.items()}], core_ids=[0])
    return r.results[0]["out_0"]
```

```python
from contextlib import ExitStack

import concourse.bass as bass
from concourse import mybir

P = 128
D = 128
CH = 512
IB = CH // P
EPS = 1e-5
SLOPE = 0.2
STEEP = float(2 ** 30)
H0, HD0 = 2, 64
H1, HD1 = 8, 16
K0 = HD0 + 1
K1 = HD1 + 1
PARTS = 3
JP = 8
GJ0 = 2
GJ1 = 4
SLOTS = 4
S0 = 2
AHEAD = 2
LATE = 7
WIDE = 2
CW = WIDE * CH
IW = WIDE * IB


def gat_kernel(nc, x, adj, W1, b1, W2, b2, W3, W3T, b3, a, Ww, WwT, Wb, aw, ab, ident_in, sel_in, out):
    f32, bf16, fp8, i32, u8 = mybir.dt.float32, mybir.dt.bfloat16, mybir.dt.float8e4, mybir.dt.int32, mybir.dt.uint8
    ALU, ACT, AX = mybir.AluOpType, mybir.ActivationFunctionType, mybir.AxisListType
    N = x.shape[0]
    NB = N // P
    NCH = N // CH
    NP = NB // JP
    NW = N // CW
    NG0 = NB // GJ0
    NG1 = NB // GJ1
    XW = max(H0 * 2 * PARTS * K0, H1 * 2 * PARTS * K1)

    ctx = ExitStack()
    with ctx:
        ctx.enter_context(nc.allow_non_contiguous_dma(reason="small weight vectors"))

        def sb(name, shape, dt):
            return ctx.enter_context(nc.sbuf_tensor(name, shape, dt))

        def sem(name):
            return ctx.enter_context(nc.semaphore(name))

        def scratch(name, shape, dt):
            return nc.dram_tensor(name, shape, dt, kind="Internal").ap()

        s1_rows = [scratch("s1_rows0", [H0, N], f32), scratch("s1_rows1", [H1, N], f32)]
        adjT8 = scratch("adjT8", [NCH, NP, P, JP * CH], u8)
        x1_dram = scratch("x1_dram", [N, D], f32)
        h1_dram = scratch("h1_dram", [N, D], f32)
        agg_dram = scratch("agg_dram", [N, D], f32)

        Xt = sb("Xt", [P, NB * XW], bf16)
        ident = sb("ident", [P, P], f32)
        ones = sb("ones", [P, CH], f32)
        sel = sb("sel", [P, 4, 2 * K1], f32)
        minus1 = sb("minus1", [P, NB], f32)
        minus_half = sb("minus_half", [P, NB], f32)
        thr = sb("thr", [P, NB, H1], f32)
        steep_s2 = sb("steep_s2", [P, NB, H1], f32)
        Ai = sb("Ai", [P, NB, H1], f32)
        Ci = sb("Ci", [P, NB, H1], f32)
        Smax = sb("Smax", [P, 2, H1], f32)
        sumV = sb("sumV", [P, H1 * K1 if H1 * K1 > H0 * K0 else H0 * K0], f32)
        wcat = sb("wcat", [P, 128 + 2 * H1], f32)
        brow = sb("brow", [1, 128 + 2 * H1], f32)
        WORK = 22656
        work = sb("work", [P, WORK], f32)

        class Region:
            def __init__(self, base, size, view):
                self.at, self.end, self.view = base, size, view

            def take(self, dt, *dims):
                n = 1
                for d in dims:
                    n *= d
                words = n * {f32: 4, bf16: 2, fp8: 1}[dt] // 4
                v = self.view[:, self.at:self.at + words]
                self.at += words
                assert self.at <= self.end, (self.at, self.end)
                if dt != f32:
                    v = v.bitcast(dt)
                if len(dims) > 1:
                    names = "abcde"[:len(dims)]
                    v = v.rearrange(f"p ({' '.join(names)}) -> p {' '.join(names)}",
                                    **{m: d for m, d in zip(names[1:], dims[1:])})
                return v

        r = Region(0, WORK, work)
        hT = r.take(f32, NB * P)
        tail = r.at
        x_all = r.take(f32, NB, D)
        r.at = tail
        V32 = r.take(f32, NB, 128 + 2 * H1)
        bexp = r.take(f32, NB, H1, 2)
        zrow = r.take(f32, NB, H1)
        mrow = r.take(f32, NB, H1)
        stat = r.take(f32, 2, NB)
        xr = Region(0, NB * XW // 2, Xt[:, :].bitcast(f32))
        sq = xr.take(f32, NB, D)
        s1_sb = xr.take(f32, N)
        wn = [xr.take(f32, D), xr.take(f32, D)]
        ablk = [xr.take(f32, H1), xr.take(f32, H1)]
        bcol = [xr.take(f32, 1), xr.take(f32, 1)]
        abrow = xr.take(f32, H1)
        XG = 4
        r2 = Region(0, NB * P, work)
        xf = [r2.take(f32, XG * XW // PARTS) for _ in range(2)]
        r = Region(0, WORK, work)
        nat = [r.take(bf16, IB, JP * P) for _ in range(S0)]
        adjT = [r.take(bf16, JP, CH) for _ in range(S0)]
        mplus = [[r.take(bf16, GJ0, CH) for _ in range(H0)] for _ in range(SLOTS)]
        mminus = [[r.take(bf16, GJ0, CH) for _ in range(H0)] for _ in range(SLOTS)]
        small = [r.take(fp8, JP, CH) for _ in range(2)]
        s1bc0 = r.take(f32, H0, CH)
        stage0 = r.take(f32, IB, H0, 2 * PARTS * K0)
        r = Region(0, WORK, work)
        adj8 = [r.take(fp8, WIDE, JP, CH) for _ in range(SLOTS)]
        mask8 = [r.take(fp8, 2, WIDE, GJ1, CH) for _ in range(SLOTS)]
        s1bcA = r.take(f32, CW)
        s1bcD = r.take(f32, CW)
        stage1 = r.take(f32, 6, CH)
        comb = r.take(f32, IW, 2, 2 * K1)
        ep = r.take(f32, IW, 2, K1)
        ep2 = r.take(f32, IW, 2, K1)
        w0 = sb("w0", [P, H0, PARTS * K0], f32)
        flag0 = sb("flag0", [P, H0], f32)
        rec0 = sb("rec0", [P, H0], f32)
        x_in = sb("x_in", [P, IB, D], f32)
        r = Region(0, IB * D, x_in[:, :, :].rearrange("p i d -> p (i d)"))
        flag1 = r.take(f32, IW, 2)
        rec1 = r.take(f32, IW, 2)
        agg_sb = r.take(f32, IW, 2, HD1)
        FB = NB // 8 if NB >= 32 else NB // 4
        NF = NB // FB
        r = Region(0, WORK, work)
        fin_y = [r.take(f32, FB, D) for _ in range(2)]
        fin_h = [r.take(f32, FB, D) for _ in range(2)]
        fin_x = [r.take(f32, FB, D) for _ in range(2)]
        fin_e = [r.take(f32, FB, D) for _ in range(2)]

        bank = [ctx.enter_context(nc.psum_tensor(f"bank{i}", [P, 512], f32)) for i in range(8)]

        def bc(ap, n):
            return ap.unsqueeze(len(ap.shape)).to_broadcast([*ap.shape, n])

        block = ctx.enter_context(nc.Block())
        sync, act, dve, pe, pool = nc.sync, nc.scalar, nc.vector, nc.tensor, nc.gpsimd
        phase_end = sem("phase_end")

        passed = {id(e): sem(f"passed_{n}") for n, e in (("sp", sync), ("act", act), ("dve", dve), ("pe", pe), ("pool", pool))}

        def wait_alone(eng, s, value):
            eng.wait_ge(s, value)
            eng.sem_inc(passed[id(eng)], 1)

        def phase_over(eng, k):
            eng.drain().then_inc(phase_end, 1)
            eng.wait_ge(phase_end, 5 * k)

        xv = x.rearrange("(b p) d -> p b d", p=P)
        x1v = x1_dram.rearrange("(b p) d -> p b d", p=P)
        h1v = h1_dram.rearrange("(b p) d -> p b d", p=P)
        LG = 4
        LB = NB // LG

        class Prologue:
            def __init__(self, layer):
                self.l, self.s = layer, {}
                self.H, self.HD = (H0, HD0) if layer == 0 else (H1, HD1)
                self.K = self.HD + 1
                for name in ("w_in", "const_in", "x_arrived", "sum_done", "centred", "squared", "var_done",
                             "rstd_done", "h_done", "hT_in_psum", "u_in_psum", "u_copied",
                             "b_in_psum", "b_copied", "v_in_psum", "s1_in_psum", "s1_copied",
                             "s1_stored", "local_max", "global_max", "shifted", "b_exp", "ac_ready", "ac_exp",
                             "sumv_in_psum", "xf_ready", "hi_done", "rest1", "mid_done", "lo_done",
                             "dve_step", "h_stored", "consts"):
                    self.s[name] = sem(f"l{layer}_{name}")
                self.x_in = [sem(f"l{layer}_x_in{g}") for g in range(LG)]
                self.VW = 128 + 2 * self.H
                self.n_t = NB // 4
                self.n_v = NB // 2
                self.n_s = N // 512
                self.groups = NB // XG

                for name in ("hT_copied", "v_copied", "s1_copied"):
                    self.s[name] = [sem(f"l{layer}_{name}_{e}") for e in ("act", "dve")]

            def views(self):
                H, K = self.H, self.K
                vw = V32[:, :, 0:self.VW]
                return vw[:, :, 0:128], vw[:, :, 128:128 + H], vw[:, :, 128 + H:128 + 2 * H]

        def copied(eng, sems, n):
            for who in range(2):
                if (n + 1 - who) // 2:
                    eng.wait_ge(sems[who], (n + 1 - who) // 2)

        def xparts(p, g):
            w = p.H * 2 * PARTS * p.K
            v = Xt[:, g * XG * w:(g + 1) * XG * w]
            return v.rearrange("p (m t k) -> p m t k", t=PARTS, k=p.K)

        def xf_view(p, g):
            v = xf[g % 2][:, 0:XG * p.H * 2 * p.K]
            return v.rearrange("p (m k) -> p m k", k=p.K)

        def pro_sync(p):
            if p.l == 0:
                sync.dma_start(ident[:, :], ident_in).then_inc(p.s["const_in"], 16)
                sync.dma_start(sel[:, :, :], sel_in).then_inc(p.s["const_in"], 16)
            src = xv if p.l == 0 else x1v
            for g in range(LG):
                sync.dma_start(x_all[:, g * LB:(g + 1) * LB, :], src[:, g * LB:(g + 1) * LB, :]).then_inc(p.x_in[g], 16)
            H, HD = p.H, p.HD
            mats = (W1, W2) if p.l == 0 else (Ww, Ww)
            biases = (b1, b2) if p.l == 0 else (Wb, Wb)
            for k in range(2):
                sync.dma_start(wn[k], mats[k]).then_inc(p.s["w_in"], 16)
                sync.dma_start(bcol[k], biases[k].rearrange("(p o) -> p o", o=1)).then_inc(p.s["w_in"], 16)
            sync.dma_start(wcat[:, 0:128], W3T if p.l == 0 else WwT).then_inc(p.s["w_in"], 16)
            sync.dma_start(brow[:, 0:128], (b3 if p.l == 0 else Wb).rearrange("(o n) -> o n", o=1)).then_inc(p.s["w_in"], 16)
            sync.wait_ge(p.s["consts"], 1)
            for k in range(2):
                for h in range(H):
                    row = (a[h, k * HD:(k + 1) * HD] if p.l == 0 else aw[0, k * HD:(k + 1) * HD])
                    sync.dma_start(ablk[k][h * HD:(h + 1) * HD, h:h + 1],
                                   row.rearrange("(p o) -> p o", o=1)).then_inc(p.s["w_in"], 16)
            if p.l == 1:
                sync.dma_start(abrow[0:1, 0:1], ab.rearrange("(o n) -> o n", o=1)).then_inc(p.s["w_in"], 16)
                for g in range(LG):
                    sync.wait_ge(p.s["h_done"], (g + 1) * LB)
                    sync.dma_start(h1v[:, g * LB:(g + 1) * LB, :],
                                   x_all[:, g * LB:(g + 1) * LB, :]).then_inc(p.s["h_stored"], 16)
            copied(sync, p.s["s1_copied"], p.n_s)
            sync.dma_start(s1_rows[p.l], s1_sb[0:H, :]).then_inc(p.s["s1_stored"], 16)
            sync.wait_ge(p.s["s1_stored"], 16)
            if p.l == 1:
                sync.wait_ge(p.s["h_stored"], 16 * LG)

        def n_weights(p):
            return 16 * (6 + 2 * p.H + (p.l == 1))

        def pro_pool(p):
            H, HD, K = p.H, p.HD, p.K
            if p.l == 0:
                pool.memset(ones[:, :], 1.0)
                pool.memset(minus1[:, :], -1.0)
                pool.memset(minus_half[:, :], -0.5)
            pool.memset(ablk[0], 0.0)
            pool.memset(ablk[1], 0.0)
            pool.memset(sumV[:, :], float(N)).then_inc(p.s["consts"], 1)
            pool.wait_ge(p.s["consts"], 1)
            for g in range(LG):
                pool.wait_ge(p.s["var_done"], g + 1)
                s = slice(g * LB, (g + 1) * LB)
                pool.tensor_tensor(stat[:, 1, s], stat[:, 1, s], minus_half[:, s], ALU.pow).then_inc(p.s["rstd_done"], 1)
            pool.wait_ge(p.s["local_max"], 1)
            pool.partition_all_reduce(Smax[:, 1, 0:H], Smax[:, 0, 0:H], P, bass.bass_isa.ReduceOp.max).then_inc(p.s["global_max"], 1)
            pool.wait_ge(p.s["b_exp"], 4)
            copied(pool, p.s["v_copied"], p.n_v)
            pool.wait_ge(p.s["s1_in_psum"], p.n_s)
            Vv, _, _ = p.views()
            for g in range(p.groups):
                if g >= 2:
                    pool.wait_ge(p.s["lo_done"], g - 1)
                o = xf_view(p, g).rearrange("p (b h t) k -> p b h t k", h=H, t=2)
                bl = slice(g * XG, (g + 1) * XG)
                for b in range(XG):
                    for t in range(2):
                        w = bexp[:, g * XG + b, 0:H, t]
                        pool.tensor_tensor(o[:, b, :, t, 0:HD], Vv[:, g * XG + b, :].rearrange("p (h d) -> p h d", h=H),
                                           bc(w, HD), ALU.mult)
                    last = pool.tensor_copy(o[:, b, :, :, HD], bexp[:, g * XG + b, 0:H, :])
                last.then_inc(p.s["xf_ready"], 1)

        def pro_dve(p):
            H, HD, K = p.H, p.HD, p.K
            steps = [0]

            def chain(ins):
                steps[0] += 1
                ins.then_inc(p.s["dve_step"], 1)
                dve.wait_ge(p.s["dve_step"], steps[0])

            for g in range(LG):
                s = slice(g * LB, (g + 1) * LB)
                xg = x_all[:, s, :]
                dve.wait_ge(p.x_in[g], 16)
                chain(nc.vector.reduce_sum(stat[:, 0, s], xg, axis=AX.X))
                chain(nc.vector.tensor_scalar(stat[:, 0, s], stat[:, 0, s], 1.0 / D, None, ALU.mult))
                nc.vector.tensor_tensor(xg, xg, bc(stat[:, 0, s], D), ALU.subtract).then_inc(p.s["centred"], 1)
                dve.wait_ge(p.s["squared"], g + 1)
                chain(nc.vector.reduce_sum(stat[:, 1, s], sq[:, s, :], axis=AX.X))
                nc.vector.tensor_scalar(stat[:, 1, s], stat[:, 1, s], 1.0 / D, EPS, ALU.mult, ALU.add).then_inc(p.s["var_done"], 1)
            for g in range(LG):
                dve.wait_ge(p.s["rstd_done"], g + 1)
                for b in range(g * LB, (g + 1) * LB):
                    nc.vector.tensor_scalar(x_all[:, b, :], x_all[:, b, :], stat[:, 1, b:b + 1], 0.0,
                                            ALU.mult, ALU.max).then_inc(p.s["h_done"], 1)
            pro_copies(p, 1)
            Vv, s2v, s1v = p.views()
            copied(dve, p.s["v_copied"], p.n_v)
            nc.vector.tensor_reduce(Smax[:, 0, 0:H], s2v.rearrange("p b h -> p h b"), axis=AX.X, op=ALU.max).then_inc(p.s["local_max"], 1)
            nc.vector.tensor_scalar(thr[:, :, 0:H], s2v, -1.0, None, ALU.mult)
            nc.vector.tensor_scalar(steep_s2[:, :, 0:H], s2v, STEEP, None, ALU.mult)
            dve.wait_ge(p.s["global_max"], 1)
            S = Smax[:, 1, 0:H].unsqueeze(1).to_broadcast([P, NB, H])
            nc.vector.tensor_tensor(mrow[:, :, 0:H], s2v, S, ALU.subtract).then_inc(p.s["shifted"], 1)
            chain(nc.vector.tensor_tensor(zrow[:, :, 0:H], s1v, S, ALU.add))
            chain(nc.vector.scalar_tensor_tensor(out=Ai[:, :, 0:H], in0=zrow[:, :, 0:H], scalar=SLOPE, in1=zrow[:, :, 0:H],
                                                 op0=ALU.mult, op1=ALU.max))
            nc.vector.scalar_tensor_tensor(out=Ci[:, :, 0:H], in0=zrow[:, :, 0:H], scalar=SLOPE, in1=Ai[:, :, 0:H],
                                           op0=ALU.mult, op1=ALU.subtract)
            chain(nc.vector.tensor_tensor(zrow[:, :, 0:H], zrow[:, :, 0:H], Ai[:, :, 0:H], ALU.subtract))
            nc.vector.tensor_copy(Ai[:, :, 0:H], zrow[:, :, 0:H]).then_inc(p.s["ac_ready"], 1)
            dve.wait_ge(p.s["sumv_in_psum"], 1)
            dve.wait_ge(p.s["consts"], 1)
            nc.vector.tensor_copy(sumV[:, 0:H * K].rearrange("p (h k) -> p h k", k=K)[:, :, 0:HD],
                                  bank[7][:, 0:128].rearrange("p (h d) -> p h d", d=HD))
            for g in range(p.groups):
                o, xs = xf_view(p, g), xparts(p, g)
                dve.wait_ge(p.s["hi_done"], g + 1)
                nc.vector.tensor_tensor(o, o, xs[:, :, 0, :], ALU.subtract).then_inc(p.s["rest1"], 1)
                dve.wait_ge(p.s["mid_done"], g + 1)
                nc.vector.tensor_tensor(xs[:, :, 2, :], o, xs[:, :, 1, :], ALU.subtract).then_inc(p.s["lo_done"], 1)

        def pro_copies(p, who):
            def copy(o, i):
                return nc.scalar.copy(o, i) if who == 0 else nc.vector.tensor_copy(o, i)
            eng = act if who == 0 else dve
            for t in range(p.n_t):
                if t % 2 == who:
                    eng.wait_ge(p.s["hT_in_psum"], t + 1)
                    copy(hT[:, t * 512:(t + 1) * 512], bank[t % 4][:, :]).then_inc(p.s["hT_copied"][who], 1)
            if who == 0:
                eng.wait_ge(p.s["u_in_psum"], 1)
                copy(wcat[:, 128:p.VW], bank[4][:, 0:2 * p.H]).then_inc(p.s["u_copied"], 1)
                eng.wait_ge(p.s["b_in_psum"], 1)
                copy(brow[:, 128:p.VW], bank[5][0:1, 0:2 * p.H]).then_inc(p.s["b_copied"], 1)
            for t in range(p.n_v):
                if t % 2 == who:
                    eng.wait_ge(p.s["v_in_psum"], t + 1)
                    copy(V32[:, 2 * t:2 * t + 2, 0:p.VW],
                         bank[t % 4][:, 0:2 * p.VW].rearrange("p (b n) -> p b n", b=2)).then_inc(p.s["v_copied"][who], 1)
            for t in range(p.n_s):
                if t % 2 == who:
                    eng.wait_ge(p.s["s1_in_psum"], t + 1)
                    copy(s1_sb[0:p.H, t * 512:(t + 1) * 512], bank[4 + t % 2][0:p.H, :]).then_inc(p.s["s1_copied"][who], 1)

        def pro_act(p):
            H, HD, K = p.H, p.HD, p.K
            for g in range(LG):
                s = slice(g * LB, (g + 1) * LB)
                act.wait_ge(p.s["centred"], g + 1)
                nc.scalar.activation(sq[:, s, :], x_all[:, s, :], ACT.Square).then_inc(p.s["squared"], 1)
            pro_copies(p, 0)
            act.wait_ge(p.s["shifted"], 1)
            for e in range(2):
                for t in range(2):
                    power = (t + e * p.l) % 2
                    nc.scalar.activation(bexp[:, :, e:H:2, t], mrow[:, :, e:H:2], ACT.Exp,
                                         scale=SLOPE if power else 1.0).then_inc(p.s["b_exp"], 1)
            act.wait_ge(p.s["ac_ready"], 1)
            nc.scalar.activation(Ai[:, :, 0:H], Ai[:, :, 0:H], ACT.Exp)
            nc.scalar.activation(Ci[:, :, 0:H], Ci[:, :, 0:H], ACT.Exp).then_inc(p.s["ac_exp"], 1)
            act.wait_ge(p.s["s1_stored"], 16)
            for g in range(p.groups):
                o, xs = xf_view(p, g), xparts(p, g)
                act.wait_ge(p.s["xf_ready"], g + 1)
                nc.scalar.copy(xs[:, :, 0, :], o).then_inc(p.s["hi_done"], 1)
                act.wait_ge(p.s["rest1"], g + 1)
                nc.scalar.copy(xs[:, :, 1, :], o).then_inc(p.s["mid_done"], 1)

        def pro_pe(p):
            H, HD, K = p.H, p.HD, p.K
            pe.wait_ge(pro[0].s["const_in"], 32)
            pe.wait_ge(pro[0].s["consts"], 1)
            pe.wait_ge(p.s["w_in"], n_weights(p))
            for k, o in ((1, 0), (0, H)):
                last = nc.tensor.matmul(bank[4][:, o:o + H], wn[k], ablk[k][:, 0:H], start=True, stop=True)
            last.then_inc(p.s["u_in_psum"], 1)
            nc.tensor.matmul(bank[5][0:1, 0:H], bcol[1], ablk[1][:, 0:H], start=True, stop=True)
            last = nc.tensor.matmul(bank[5][0:1, H:2 * H], bcol[0], ablk[0][:, 0:H], start=True, stop=p.l == 0)
            if p.l == 1:
                last = nc.tensor.matmul(bank[5][0:1, H:2 * H], ones[0:1, 0:1], abrow[0:1, 0:1].to_broadcast([1, H]), start=False, stop=True)
            last.then_inc(p.s["b_in_psum"], 1)
            for t in range(p.n_t):
                pe.wait_ge(p.s["h_done"], 4 * t + 4)
                if t >= 4:
                    copied(pe, p.s["hT_copied"], t - 3)
                for b in range(4):
                    last = nc.tensor.transpose(bank[t % 4][:, b * P:(b + 1) * P], x_all[:, 4 * t + b, :], ident[:, :])
                last.then_inc(p.s["hT_in_psum"], 1)
            copied(pe, p.s["hT_copied"], p.n_t)
            pe.wait_ge(p.s["u_copied"], 1)
            pe.wait_ge(p.s["b_copied"], 1)
            if p.l == 1:
                pe.wait_ge(p.s["h_stored"], 16 * LG)
            for t in range(p.n_v):
                if t >= 4:
                    copied(pe, p.s["v_copied"], t - 3)
                for b in range(2):
                    o = bank[t % 4][:, b * p.VW:(b + 1) * p.VW]
                    nc.tensor.matmul(o, ones[0:1, 0:P], brow[0:1, 0:p.VW], start=True, stop=False)
                    last = nc.tensor.matmul(o, hT[:, (2 * t + b) * P:(2 * t + b + 1) * P], wcat[:, 0:p.VW],
                                            start=False, stop=True)
                last.then_inc(p.s["v_in_psum"], 1)
            for t in range(p.n_s):
                if t >= 2:
                    copied(pe, p.s["s1_copied"], t - 1)
                o = bank[4 + t % 2][0:H, :]
                nc.tensor.matmul(o, brow[0:1, 128 + H:p.VW], ones[0:1, :], start=True, stop=False)
                nc.tensor.matmul(o, wcat[:, 128 + H:p.VW], hT[:, t * 512:(t + 1) * 512],
                                 start=False, stop=True).then_inc(p.s["s1_in_psum"], 1)
            copied(pe, p.s["v_copied"], p.n_v)
            for b in range(NB):
                last = nc.tensor.matmul(bank[7][:, 0:128], ones[:, 0:P], V32[:, b, 0:128], start=b == 0, stop=b == NB - 1)
            last.then_inc(p.s["sumv_in_psum"], 1)

        pro = [Prologue(0), Prologue(1)]

        adj_v = adj.rearrange("(c i p) (q j) -> c q p i j", i=IB, p=P, j=JP * P)
        xchunk = x.rearrange("(c i p) d -> c p i d", i=IB, p=P)
        x1chunk = x1_dram.rearrange("(c i p) d -> c p i d", i=IB, p=P)
        s1row0 = s1_rows[0].rearrange("h (c n) -> c h n", n=CH)
        nat_in = [sem(f"nat_in{s}") for s in range(S0)]
        transposed = [sem(f"transposed{s}") for s in range(S0)]
        shrunk = [sem(f"shrunk{s}") for s in range(S0)]
        mask_stored = [sem(f"mask_stored{s}") for s in range(2)]
        s1bc_in = sem("s1bc_in")
        side_ready0 = sem("side_ready0")
        plus_ready0 = sem("plus_ready0")
        minus_ready0 = sem("minus_ready0")
        masks_free0 = sem("masks_free0")
        sums_ready0 = sem("sums_ready0")
        bank_free0 = [sem("bank_free0_act"), sem("bank_free0_dve")]
        stage_free0 = sem("stage_free0")
        x_chunk_in = sem("x_chunk_in")
        x1_ready = sem("x1_ready")
        x1_stored = sem("x1_stored")
        pool_step0 = sem("pool_step0")
        X0 = Xt[:, 0:NB * H0 * 2 * PARTS * K0].rearrange("p (b h t k) -> p b h t k", h=H0, t=2, k=PARTS * K0)

        def at(c, per, k):
            return c * per + k

        def side0(c, k):
            act.wait_ge(masks_free0, at(c, NG0, k + 1))
            for h in range(H0):
                for j in range(GJ0):
                    last = nc.scalar.activation(mplus[k % SLOTS][h][:, j, :], s1bc0[:, h, :], ACT.Sigmoid, scale=STEEP,
                                                bias=steep_s2[:, k * GJ0 + j, h:h + 1])
                last.then_inc(side_ready0, 1)

        def s1_load0(c):
            act.dma_start(s1bc0, s1row0[c].unsqueeze(0).to_broadcast([P, H0, CH])).then_inc(s1bc_in, 16)

        def copy_out0(c, who):
            eng, copy = (act, nc.scalar.copy) if who == 0 else (dve, nc.vector.tensor_copy)
            eng.wait_ge(stage_free0, at(c, IB, IB))
            for n in range(4):
                i, h = 2 * who + n // 2, n % 2
                if 4 * who + n < 7:
                    eng.wait_ge(sums_ready0, at(c, 7, 4 * who + n + 1))
                else:
                    eng.wait_ge(masks_free0, at(c, NG0, NG0 + SLOTS))
                copy(stage0[:, i, h, :], bank[4 * who + n][:, 0:2 * PARTS * K0]).then_inc(bank_free0[who], 1)

        def main0_act():
            act.sem_inc(bank_free0[0], 4)
            s1_load0(0)
            act.wait_ge(s1bc_in, 16)
            for k in range(AHEAD):
                side0(0, k)

            def chunk(c, more):
                for k in range(AHEAD, NG0):
                    side0(c, k)
                if more:
                    act.wait_ge(side_ready0, at(c, 2 * NG0, 2 * NG0))
                    s1_load0(c + 1)
                    act.wait_ge(s1bc_in, at(c, 16, 32))
                    for k in range(AHEAD):
                        side0(c + 1, k)
                copy_out0(c, 0)

            with act.Fori(0, NCH - 1) as c:
                chunk(c, True)
            chunk(NCH - 1, False)

        def masks0(c, k):
            q, half = k * GJ0 // JP, k * GJ0 % JP
            if half == 0:
                dve.wait_ge(transposed[q % S0], at(c, 64 * NP // S0, 64 * (q // S0 + 1)))
            m0 = adjT[q % S0][:, half:half + GJ0, :]
            for h in range(H0):
                dve.wait_ge(side_ready0, at(c, 2 * NG0, 2 * k + h + 1))
                m = mplus[k % SLOTS][h]
                nc.vector.tensor_tensor(m, m, m0, ALU.mult).then_inc(plus_ready0, 1)
            for h in range(H0):
                dve.wait_ge(plus_ready0, at(c, 2 * NG0, 2 * k + h + 1))
                nc.vector.tensor_tensor(mminus[k % SLOTS][h], m0, mplus[k % SLOTS][h], ALU.subtract).then_inc(minus_ready0, 1)

        def main0_dve():
            dve.sem_inc(bank_free0[1], 4)
            for k in range(AHEAD):
                masks0(0, k)

            def chunk(c, more):
                for k in range(AHEAD, NG0):
                    masks0(c, k)
                if more:
                    for k in range(AHEAD):
                        masks0(c + 1, k)
                copy_out0(c, 1)

            with dve.Fori(0, NCH - 1) as c:
                chunk(c, True)
            chunk(NCH - 1, False)

        def main0_pe():
            pe.sem_inc(masks_free0, SLOTS)
            with pe.Fori(0, NCH) as c:
                for k in range(NG0):
                    pe.wait_ge(plus_ready0, at(c, 2 * NG0, 2 * k + 2))
                    pe.wait_ge(minus_ready0, at(c, 2 * NG0, 2 * k + 2))
                    for j in range(GJ0):
                        b = k * GJ0 + j
                        for i in range(IB):
                            for h in range(H0):
                                n = 2 * i + h
                                if b == 0:
                                    pe.wait_ge(bank_free0[n // 4], at(c, 4, n % 4 + 1))
                                for t, m in enumerate((mplus, mminus)):
                                    last = nc.tensor.matmul(
                                        bank[n][:, t * PARTS * K0:(t + 1) * PARTS * K0],
                                        m[k % SLOTS][h][:, j, i * P:(i + 1) * P], X0[:, b, h, t, :],
                                        start=b == 0 and t == 0, stop=b == NB - 1 and t == 1, skip_group_check=True)
                                if b == NB - 1 and n < 7:
                                    last.then_inc(sums_ready0, 1)
                    last.then_inc(masks_free0, 1)

        def main0_sync():
            def piece(c, q, first):
                s = q % S0
                wait_alone(sync, nat_in[s], at(c, 16 * NP // S0, 16 * (q // S0 + 1)))
                if not (first and q < S0):
                    wait_alone(sync, minus_ready0, at(c, 2 * NG0, 2 * (q - S0 + 1) * JP // GJ0))
                    wait_alone(sync, shrunk[s], at(c, 16 * NP // S0, 16 * (q // S0)))
                for i in range(IB):
                    sync.dma_start_transpose(adjT[s][:, :, i * P:(i + 1) * P], nat[s][:, i, :]).then_inc(transposed[s], 16)

            def store(c, q):
                wait_alone(sync, shrunk[q % S0], at(c, 16 * NP // S0, 16 * (q // S0 + 1)))
                sync.dma_start(adjT8[c, q], small[q % 2].rearrange("p j n -> p (j n)").bitcast(u8)).then_inc(mask_stored[q % 2], 16)

            for q in range(NP):
                piece(0, q, True)
                if q >= 2:
                    store(0, q - 2)
            with sync.Fori(1, NCH) as c:
                for q in range(NP):
                    piece(c, q, False)
                    if q < 2:
                        store(c - 1, NP + q - 2)
                    else:
                        store(c, q - 2)
            for q in (NP - 2, NP - 1):
                store(NCH - 1, q)
            for s in range(2):
                sync.wait_ge(mask_stored[s], 16 * NCH * NP // 2)

        def main0_pool():
            steps = [0]
            EPS_PER = 9

            def load(c, q, first):
                s = q % S0
                if not (first and q < S0):
                    wait_alone(pool, transposed[s], at(c, 64 * NP // S0, 64 * (q // S0)))
                pool.dma_start(nat[s], adj_v[c, q]).then_inc(nat_in[s], 16)

            def shrink(c, q, first):
                s = q % S0
                wait_alone(pool, transposed[s], at(c, 64 * NP // S0, 64 * (q // S0 + 1)))
                if not (first and q < 2):
                    wait_alone(pool, mask_stored[q % 2], at(c, 16 * NP // 2, 16 * (q // 2)))
                pool.dma_start(small[q % 2], adjT[s]).then_inc(shrunk[s], 16)

            def norm(c, i):
                n = [0]

                def chain(ins):
                    n[0] += 1
                    ins.then_inc(pool_step0, 1)
                    wait_alone(pool, pool_step0, at(c, 10 * IB, 10 * i + n[0]))

                if i == 0:
                    pool.dma_start(x_in[:, :, :], xchunk[c]).then_inc(x_chunk_in, 16)
                for who in range(2):
                    if i == 2 * who:
                        wait_alone(pool, bank_free0[who], at(c, 4, 8))
                bi = c * IB + i
                st = stage0[:, i, :, :].rearrange("p h (t k) -> p h t k", t=2)
                plus, minus = st[:, :, 0, :], st[:, :, 1, :]
                A = bc(Ai[:, bass.ds(bi, 1), 0:H0].rearrange("p o h -> p (o h)"), PARTS * K0)
                C = bc(Ci[:, bass.ds(bi, 1), 0:H0].rearrange("p o h -> p (o h)"), PARTS * K0)
                pool.tensor_tensor(plus, plus, A, ALU.mult)
                chain(pool.tensor_tensor(minus, minus, C, ALU.mult))
                chain(pool.tensor_tensor(w0[:, :, :], plus, minus, ALU.add))
                pool.sem_inc(stage_free0, 1)
                chain(pool.tensor_tensor(w0[:, :, 0:K0], w0[:, :, 0:K0], w0[:, :, K0:2 * K0], ALU.add))
                chain(pool.tensor_tensor(w0[:, :, 0:K0], w0[:, :, 0:K0], w0[:, :, 2 * K0:3 * K0], ALU.add))
                chain(pool.tensor_scalar(flag0[:, :], w0[:, :, HD0], 0.0, None, ALU.is_equal))
                chain(pool.tensor_tensor(w0[:, :, K0:2 * K0], sumV[:, 0:H0 * K0].rearrange("p (h k) -> p h k", k=K0),
                                         bc(flag0[:, :], K0), ALU.mult))
                chain(pool.tensor_tensor(w0[:, :, 0:K0], w0[:, :, 0:K0], w0[:, :, K0:2 * K0], ALU.add))
                chain(pool.tensor_tensor(rec0[:, :], w0[:, :, HD0], minus1[:, 0:H0], ALU.pow))
                chain(pool.tensor_tensor(w0[:, :, 0:HD0], w0[:, :, 0:HD0], bc(rec0[:, :], HD0), ALU.mult))
                if i == 0:
                    wait_alone(pool, x_chunk_in, at(c, 16, 16))
                chain(pool.tensor_tensor(x_in[:, i, :].rearrange("p (h d) -> p h d", h=H0),
                                         x_in[:, i, :].rearrange("p (h d) -> p h d", h=H0), w0[:, :, 0:HD0], ALU.add))
                if i == IB - 1:
                    pool.dma_start(x1chunk[c], x_in[:, :, :]).then_inc(x1_stored, 16)
                    wait_alone(pool, x1_stored, at(c, 16, 16))

            when = {NP // IB * i + NP // IB - 1: i for i in range(IB)}

            def chunk(c, first):
                for q in range(NP):
                    load(c, q, first)
                    if q >= 2:
                        shrink(c, q - 2, first)
                    elif not first:
                        shrink(c - 1, NP + q - 2, False)
                    if not first and q in when:
                        norm(c - 1, when[q])

            pool.sem_inc(stage_free0, IB)
            chunk(0, True)
            with pool.Fori(1, NCH) as c:
                chunk(c, False)
            for q in (NP - 2, NP - 1):
                shrink(NCH - 1, q, False)
            for i in range(IB):
                norm(NCH - 1, i)
            pool.wait_ge(x1_stored, 16 * NCH)

        adj8_v = adjT8.rearrange("(c a) q p n -> c q p a n", a=WIDE)
        s1row1 = s1_rows[1].rearrange("h (c n) -> c h n", n=CW)
        aggchunk = agg_dram.rearrange("(c i p) (h d) -> c p i h d", i=IW, p=P, d=HD1)
        X1 = Xt[:, 0:NB * H1 * 2 * PARTS * K1].rearrange("p (b k) -> p b k", b=NB)
        M1 = 2 * PARTS * K1
        PER_GROUP = JP // GJ1
        s1A_in = sem("s1A_in")
        s1D_in = sem("s1D_in")
        adj_in = [sem(f"adj_in{s}") for s in range(SLOTS)]
        side_act = sem("side_act")
        side_dve = sem("side_dve")
        mask_ready = sem("mask_ready")
        masks_free = sem("masks_free")
        sums_ready = sem("sums_ready")
        bank_free = [sem("bank_free_act"), sem("bank_free_dve")]
        combined = sem("combined")
        comb_copied = sem("comb_copied")
        comb_free = sem("comb_free")
        agg_step = sem("agg_step")
        agg_stored = sem("agg_stored")
        ORDER = ((0, 1, 4), (2, 3, 5))

        class Sweep:
            def __init__(self, w):
                self.w, self.h = w, 2 * w
                self.c0, self.c1 = w * NW, (w + 1) * NW

        sweeps = [Sweep(w) for w in range(H1 // 2)]

        def sweep_loops(eng, chunk):
            for n, w in enumerate(sweeps):
                with eng.Fori(w.c0, w.c1 - 1) as c:
                    chunk(w, c, (w, c + 1))
                chunk(w, w.c1 - 1, (sweeps[n + 1], w.c1) if n + 1 < len(sweeps) else None)

        def s1_load(w, c, who):
            eng, dst, done = ((act, s1bcA, s1A_in), (sync, s1bcD, s1D_in))[who]
            eng.dma_start(dst, s1row1[c - w.c0, w.h + who].unsqueeze(0).to_broadcast([P, CW])).then_inc(done, 16)

        def side1_act(w, c, k):
            wait_alone(act, masks_free, at(c, NG1, k + 1))
            for j in range(GJ1):
                last = nc.scalar.activation(mask8[k % SLOTS][:, 0, :, j, :], s1bcA.rearrange("p (a n) -> p a n", a=WIDE),
                                            ACT.Sigmoid, scale=STEEP,
                                            bias=steep_s2[:, k * GJ1 + j, w.h:w.h + 1], saturate=False)
            last.then_inc(side_act, 1)

        def copy_out1(w, c, who):
            eng, copy = (act, nc.scalar.copy) if who == 0 else (dve, nc.vector.tensor_copy)
            wait_alone(eng, combined, at(c, 1, 1))
            for b in ORDER[who]:
                if b < 5:
                    wait_alone(eng, sums_ready, at(c, 5, b + 1))
                else:
                    wait_alone(eng, masks_free, at(c, NG1, NG1 + SLOTS))
                copy(stage1[0:M1, b, :], bank[b][0:M1, :]).then_inc(bank_free[who], 1)

        def comb_out(w, c):
            wait_alone(act, comb_free, at(c, 1, 1))
            wait_alone(act, combined, at(c, 1, 2))
            for n in range(WIDE):
                nc.scalar.copy(comb[:, IB * n:IB * (n + 1), :, :].rearrange("p i h k -> p (i h k)"),
                               bank[6 + n][:, 0:IB * 2 * 2 * K1]).then_inc(comb_copied, 1)

        def main1_act():
            act.sem_inc(bank_free[0], 3)
            act.sem_inc(comb_copied, 2)
            s1_load(sweeps[0], 0, 0)
            act.wait_ge(s1A_in, 16)
            for k in range(LATE):
                side1_act(sweeps[0], 0, k)

            def chunk(w, c, following):
                for k in range(LATE, NG1):
                    side1_act(w, c, k)
                if following:
                    wait_alone(act, side_act, at(c, NG1, NG1))
                    s1_load(*following, 0)
                    wait_alone(act, s1A_in, at(c, 16, 32))
                    for k in range(AHEAD):
                        side1_act(*following, k)
                copy_out1(w, c, 0)
                if following:
                    for k in range(AHEAD, LATE):
                        side1_act(*following, k)
                comb_out(w, c)

            sweep_loops(act, chunk)

        def masks1(w, c, k):
            wait_alone(dve, masks_free, at(c, NG1, k + 1))
            for j in range(GJ1):
                last = nc.vector.tensor_scalar(mask8[k % SLOTS][:, 1, :, j, :], s1bcD.rearrange("p (a n) -> p a n", a=WIDE),
                                               thr[:, k * GJ1 + j, w.h + 1:w.h + 2], None, ALU.is_ge, saturate=False)
            last.then_inc(side_dve, 1)
            q, part = k // PER_GROUP, k % PER_GROUP
            if part == 0:
                wait_alone(dve, adj_in[q % SLOTS], at(c, 16 * NP // SLOTS, 16 * (q // SLOTS + 1)))
            m0 = adj8[q % SLOTS][:, :, part * GJ1:(part + 1) * GJ1, :].rearrange("p a j n -> p a (j n)").bitcast(i32)
            for n in range(2):
                wait_alone(dve, (side_act, side_dve)[n], at(c, NG1, k + 1))
                m = mask8[k % SLOTS][:, n, :, :, :].rearrange("p a j n -> p a (j n)").bitcast(i32)
                nc.vector.tensor_tensor(m, m, m0, ALU.bitwise_and).then_inc(mask_ready, 1)

        def main1_dve():
            dve.sem_inc(bank_free[1], 3)
            dve.wait_ge(s1D_in, 16)
            for k in range(AHEAD):
                masks1(sweeps[0], 0, k)

            def chunk(w, c, following):
                for k in range(AHEAD, NG1):
                    masks1(w, c, k)
                if following:
                    wait_alone(dve, s1D_in, at(c, 16, 32))
                    for k in range(AHEAD):
                        masks1(*following, k)
                copy_out1(w, c, 1)

            sweep_loops(dve, chunk)

        def main1_pe():
            pe.sem_inc(masks_free, SLOTS)
            pe.sem_inc(combined, 1)

            def group(w, c, k):
                wait_alone(pe, mask_ready, at(c, 2 * NG1, 2 * (k + 1)))
                q, part = k // PER_GROUP, k % PER_GROUP
                for j in range(GJ1):
                    b = k * GJ1 + j
                    for n in range(6):
                        if b == 0:
                            who = 0 if n in ORDER[0] else 1
                            wait_alone(pe, bank_free[who], at(c, 3, ORDER[who].index(n) + 1))
                        half, h = n % 2, n // 2
                        if h < 2:
                            o = (w.h + h) * M1
                            rhs = mask8[k % SLOTS][:, h, half, j, :]
                        else:
                            o = w.h * M1 + M1 // 2
                            rhs = adj8[q % SLOTS][:, half, part * GJ1 + j, :]
                        last = nc.tensor.matmul(bank[n][0:M1, :], X1[:, b, o:o + M1], rhs, start=b == 0, stop=b == NB - 1)
                        if b == NB - 1 and n < 5:
                            last.then_inc(sums_ready, 1)
                last.then_inc(masks_free, 1)

            def combine(w, c):
                for who in range(2):
                    wait_alone(pe, bank_free[who], at(c, 3, 6))
                wait_alone(pe, comb_copied, at(c, 2, 2))
                for i in range(IW):
                    half, cols = i // IB, slice(i % IB * P, (i % IB + 1) * P)
                    for h in range(2):
                        o = bank[6 + half][:, (i % IB * 2 + h) * 2 * K1:(i % IB * 2 + h + 1) * 2 * K1]
                        nc.tensor.matmul(o, stage1[0:M1, 2 * h + half, cols], sel[0:M1, h, :], start=True, stop=False)
                        last = nc.tensor.matmul(o, stage1[0:M1, 4 + half, cols], sel[0:M1, 2 + h, :],
                                                start=False, stop=True)
                last.then_inc(combined, 1)

            for k in range(AHEAD):
                group(sweeps[0], 0, k)

            def chunk(w, c, following):
                for k in range(AHEAD, NG1):
                    group(w, c, k)
                if following:
                    for k in range(AHEAD):
                        group(*following, k)
                combine(w, c)

            sweep_loops(pe, chunk)

        def main1_sync():
            def chunk(w, c, first):
                for q in range(NP):
                    s = q % SLOTS
                    if not (first and q < SLOTS):
                        wait_alone(sync, masks_free, at(c, NG1, (q - SLOTS + 1) * PER_GROUP + SLOTS))
                    sync.dma_start(adj8[s].rearrange("p a j n -> p a (j n)").bitcast(u8), adj8_v[c - w.c0, q]).then_inc(adj_in[s], 16)
                    if q == 1 and not first:
                        wait_alone(sync, side_dve, at(c, NG1, 0))
                        s1_load(w, c, 1)

            s1_load(sweeps[0], 0, 1)
            chunk(sweeps[0], 0, True)
            for w in sweeps:
                with sync.Fori(max(w.c0, 1), w.c1) as c:
                    chunk(w, c, False)

        def main1_pool():
            pool.sem_inc(comb_free, 1)
            for w in sweeps:
                with pool.Fori(w.c0, w.c1) as c:
                    n = [0]

                    def chain(ins):
                        n[0] += 1
                        ins.then_inc(agg_step, 1)
                        wait_alone(pool, agg_step, at(c, 8, n[0]))

                    wait_alone(pool, comb_copied, at(c, 2, 4))
                    for t, (src, dst) in enumerate(((Ai, ep), (Ci, ep2))):
                        scale = src[:, bass.ds((c - w.c0) * IW, IW), w.h:w.h + 2]
                        for h in range(2):
                            last = pool.tensor_tensor(dst[:, :, h, :], comb[:, :, h, t * K1:(t + 1) * K1],
                                                      bc(scale[:, :, h], K1), ALU.mult)
                        chain(last)
                    pool.sem_inc(comb_free, 1)
                    chain(pool.tensor_tensor(ep, ep, ep2, ALU.add))
                    chain(pool.tensor_scalar(flag1, ep[:, :, :, HD1], 0.0, None, ALU.is_equal))
                    for h in range(2):
                        v = sumV[:, (w.h + h) * K1:(w.h + h + 1) * K1].unsqueeze(1).to_broadcast([P, IW, K1])
                        last = pool.tensor_tensor(ep2[:, :, h, :], v, bc(flag1[:, :, h], K1), ALU.mult)
                    chain(last)
                    chain(pool.tensor_tensor(ep, ep, ep2, ALU.add))
                    chain(pool.tensor_tensor(rec1, ep[:, :, :, HD1], minus1[:, 0:IW * 2].rearrange("p (i h) -> p i h", h=2), ALU.pow))
                    chain(pool.tensor_tensor(agg_sb, ep[:, :, :, 0:HD1], bc(rec1, HD1), ALU.mult))
                    pool.dma_start(aggchunk[c - w.c0][:, :, w.h:w.h + 2, :].rearrange("p i h d -> p i (h d)"),
                                   agg_sb.rearrange("p i h d -> p i (h d)")).then_inc(agg_stored, 16)
                    wait_alone(pool, agg_stored, at(c, 16, 16))

        aggv = agg_dram.rearrange("(b p) d -> p b d", p=P)
        outv = out.rearrange("(b p) d -> p b d", p=P)
        fin_in = [sem(f"fin_in{s}") for s in range(2)]
        fin_low = sem("fin_low")
        fin_exp = sem("fin_exp")
        fin_done = sem("fin_done")
        fin_sum = sem("fin_sum")
        fin_two = sem("fin_two")
        out_stored = [sem(f"out_stored{s}") for s in range(2)]

        def fin_sync():
            def store(t):
                sync.wait_ge(fin_done, t + 1)
                sync.dma_start(outv[:, t * FB:(t + 1) * FB, :], fin_e[t % 2]).then_inc(out_stored[t % 2], 16)

            for t in range(NF):
                if t >= 2:
                    sync.wait_ge(fin_done, t - 1)
                for dst, src in ((fin_y, aggv), (fin_h, h1v), (fin_x, x1v)):
                    sync.dma_start(dst[t % 2], src[:, t * FB:(t + 1) * FB, :]).then_inc(fin_in[t % 2], 16)
                if t >= 1:
                    store(t - 1)
            store(NF - 1)
            for s in range(2):
                sync.wait_ge(out_stored[s], 16 * NF // 2)

        def fin_dve():
            for t in range(NF):
                s = t % 2
                dve.wait_ge(fin_in[s], 48 * (t // 2 + 1))
                nc.vector.tensor_tensor(fin_y[s], fin_y[s], fin_h[s], ALU.add).then_inc(fin_sum, 1)
                if t >= 2:
                    dve.wait_ge(out_stored[s], 16 * (t // 2))
                dve.wait_ge(fin_sum, t + 1)
                nc.vector.tensor_scalar(fin_h[s], fin_y[s], 0.0, None, ALU.min).then_inc(fin_low, 1)
                dve.wait_ge(fin_exp, t + 1)
                nc.vector.scalar_tensor_tensor(out=fin_y[s], in0=fin_y[s], scalar=0.0, in1=fin_e[s],
                                               op0=ALU.max, op1=ALU.add).then_inc(fin_two, 1)
                dve.wait_ge(fin_two, t + 1)
                nc.vector.scalar_tensor_tensor(out=fin_e[s], in0=fin_y[s], scalar=-1.0, in1=fin_x[s],
                                               op0=ALU.add, op1=ALU.add).then_inc(fin_done, 1)

        def fin_act():
            for t in range(NF):
                act.wait_ge(fin_low, t + 1)
                nc.scalar.activation(fin_e[t % 2], fin_h[t % 2], ACT.Exp).then_inc(fin_exp, 1)

        @block.sync
        def _(eng):
            pro_sync(pro[0])
            phase_over(eng, 1)
            main0_sync()
            phase_over(eng, 2)
            pro_sync(pro[1])
            phase_over(eng, 3)
            main1_sync()
            phase_over(eng, 4)
            fin_sync()

        @block.scalar
        def _(eng):
            pro_act(pro[0])
            phase_over(eng, 1)
            main0_act()
            phase_over(eng, 2)
            pro_act(pro[1])
            phase_over(eng, 3)
            main1_act()
            phase_over(eng, 4)
            fin_act()

        @block.vector
        def _(eng):
            pro_dve(pro[0])
            phase_over(eng, 1)
            main0_dve()
            phase_over(eng, 2)
            pro_dve(pro[1])
            phase_over(eng, 3)
            main1_dve()
            phase_over(eng, 4)
            fin_dve()

        @block.tensor
        def _(eng):
            pro_pe(pro[0])
            phase_over(eng, 1)
            main0_pe()
            phase_over(eng, 2)
            pro_pe(pro[1])
            phase_over(eng, 3)
            main1_pe()
            phase_over(eng, 4)

        @block.gpsimd
        def _(eng):
            pro_pool(pro[0])
            phase_over(eng, 1)
            main0_pool()
            phase_over(eng, 2)
            pro_pool(pro[1])
            phase_over(eng, 3)
            main1_pool()
            phase_over(eng, 4)


def kernel(**inputs):
    import numpy as np
    import concourse.bacc as bacc
    from concourse import mybir
    from concourse.bass_utils import run_bass_kernel_spmd as run

    i = {k: np.ascontiguousarray(v) for k, v in inputs.items()}
    sel = np.zeros((128, 4, 2 * K1), np.float32)
    for part in range(PARTS):
        for k in range(K1):
            for e in range(2):
                sel[(e * PARTS + part) * K1 + k, e, k] = 1.0
                sel[((1 - e) * PARTS + part) * K1 + k, e, K1 + k] = -1.0
                sel[(e * PARTS + part) * K1 + k, 2 + e, K1 + k] = 1.0
    arrays = {
        "x": i["x"], "adj": i["adj"],
        "W1": i["L0_gnn_W1"], "b1": i["L0_gnn_b1"], "W2": i["L0_gnn_W2"], "b2": i["L0_gnn_b2"],
        "W3": i["L0_gnn_W3"], "W3T": np.ascontiguousarray(i["L0_gnn_W3"].T), "b3": i["L0_gnn_b3"], "a": i["L0_gnn_a"],
        "Ww": i["L1_gnn_W_w"], "WwT": np.ascontiguousarray(i["L1_gnn_W_w"].T), "Wb": i["L1_gnn_W_b"],
        "aw": i["L1_gnn_a_w"], "ab": i["L1_gnn_a_b"],
        "ident": np.eye(128, dtype=np.float32), "sel": sel,
    }
    nc = bacc.Bacc("TRN2", target_bir_lowering=False, num_devices=1)
    args = [nc.dram_tensor(f"in_{n}", v.shape, mybir.dt.from_np(v.dtype), kind="ExternalInput").ap()
            for n, v in arrays.items()]
    out = nc.dram_tensor("out_0", i["x"].shape, mybir.dt.float32, kind="ExternalOutput").ap()
    gat_kernel(nc, *args, out)
    r = run(nc, [{f"in_{n}": v for n, v in arrays.items()}], core_ids=[0])
    return r.results[0]["out_0"]
```

```python
from contextlib import ExitStack

import concourse.bass as bass
from concourse import mybir

P = 128
D = 128
CH = 512
IB = CH // P
EPS = 1e-5
SLOPE = 0.2
STEEP = float(2 ** 30)
H0, HD0 = 2, 64
H1, HD1 = 8, 16
K0 = HD0 + 1
K1 = HD1 + 1
PARTS = 3
JP = 8
GJ0 = 2
GJ1 = 4
SLOTS = 4
S0 = 2
AHEAD = 2
AHEAD0 = 1
SHARED = (3, 5, 7, 9, 11, 13)
WIDE = 2
CW = WIDE * CH
IW = WIDE * IB


def gat_kernel(nc, x, adj, W1, b1, W2, b2, W3, W3T, b3, a, Ww, WwT, Wb, aw, ab, ident_in, out):
    f32, bf16, fp8, i32, u8 = mybir.dt.float32, mybir.dt.bfloat16, mybir.dt.float8e4, mybir.dt.int32, mybir.dt.uint8
    ALU, ACT, AX = mybir.AluOpType, mybir.ActivationFunctionType, mybir.AxisListType
    N = x.shape[0]
    NB = N // P
    NCH = N // CH
    NP = NB // JP
    NW = N // CW
    NG0 = NB // GJ0
    NG1 = NB // GJ1
    XW = max(H0 * 2 * PARTS * K0, H1 * 2 * PARTS * K1)

    ctx = ExitStack()
    with ctx:
        ctx.enter_context(nc.allow_non_contiguous_dma(reason="small weight vectors"))

        def sb(name, shape, dt):
            return ctx.enter_context(nc.sbuf_tensor(name, shape, dt))

        def sem(name):
            return ctx.enter_context(nc.semaphore(name))

        def scratch(name, shape, dt):
            return nc.dram_tensor(name, shape, dt, kind="Internal").ap()

        s1_rows = [scratch("s1_rows0", [H0, N], f32), scratch("s1_rows1", [H1, N], f32)]
        adjT8 = scratch("adjT8", [NCH, NP, P, JP * CH], u8)
        x1_dram = scratch("x1_dram", [N, D], f32)
        h1_dram = scratch("h1_dram", [N, D], f32)
        agg_dram = scratch("agg_dram", [N, D], f32)

        Xt = sb("Xt", [P, NB * XW], bf16)
        ident = sb("ident", [P, P], f32)
        ones = sb("ones", [P, P], f32)
        minus1 = sb("minus1", [P, NB], f32)
        minus_half = sb("minus_half", [P, NB], f32)
        thr = sb("thr", [P, NB, H1], f32)
        steep_s2 = sb("steep_s2", [P, NB, H1], f32)
        Ai = sb("Ai", [P, NB, H1], f32)
        Ci = sb("Ci", [P, NB, H1], f32)
        Smax = sb("Smax", [P, H1], f32)
        sumV = sb("sumV", [P, H1 * K1 if H1 * K1 > H0 * K0 else H0 * K0], f32)
        wcat = [sb(f"wcat{l}", [P, 128 + 2 * h], f32) for l, h in enumerate((H0, H1))]
        ball = [sb(f"ball{l}", [P, 128 + 2 * h], f32) for l, h in enumerate((H0, H1))]
        bias_col = [sb(f"bias_col{l}", [P, 1], f32) for l in range(2)]
        WORK = 22656
        work = sb("work", [P, WORK], f32)

        class Region:
            def __init__(self, base, size, view):
                self.at, self.end, self.view = base, size, view

            def take(self, dt, *dims):
                n = 1
                for d in dims:
                    n *= d
                words = n * {f32: 4, bf16: 2, fp8: 1}[dt] // 4
                v = self.view[:, self.at:self.at + words]
                self.at += words
                assert self.at <= self.end, (self.at, self.end)
                if dt != f32:
                    v = v.bitcast(dt)
                if len(dims) > 1:
                    names = "abcde"[:len(dims)]
                    v = v.rearrange(f"p ({' '.join(names)}) -> p {' '.join(names)}",
                                    **{m: d for m, d in zip(names[1:], dims[1:])})
                return v

        XG = 2
        XS = 6
        r = Region(0, WORK, work)
        hT = r.take(f32, NB * P)
        tail = r.at
        x_all = r.take(f32, NB, D)
        r.at = tail
        V32 = r.take(f32, NB, 128 + 2 * H1)
        stat = r.take(f32, 2, NB)
        bexp = r.take(f32, NB, H1, 2)
        xf = [r.take(f32, XG * XW // PARTS) for _ in range(XS)]
        xr = Region(0, NB * XW // 2, Xt[:, :].bitcast(f32))
        sq = xr.take(f32, NB, D)
        rows_sb = xr.take(f32, N)
        wn = [[xr.take(f32, D) for _ in range(2 - l)] for l in range(2)]
        ablk = [[xr.take(f32, h) for _ in range(2)] for h in (H0, H1)]
        bcol = [[xr.take(f32, 1) for _ in range(2 - l)] for l in range(2)]
        brow = [xr.take(f32, 128 + 2 * h) for h in (H0, H1)]
        abrow = xr.take(f32, 1)
        rowmax = xr.take(f32, 5)
        hsum = xr.take(f32, N // 512 + 1)
        xr2 = Region(NB * XW // 8 * 3 + 512, NB * XW // 2, Xt[:, :].bitcast(f32))
        dexp = xr2.take(f32, NB, H1)
        zrow = xr2.take(f32, NB, H1)
        mrow = xr2.take(f32, NB, H1)
        r = Region(0, WORK, work)
        nat = [r.take(bf16, IB, JP * P) for _ in range(S0)]
        adjT = [r.take(bf16, JP, CH) for _ in range(S0)]
        mplus = [[r.take(bf16, GJ0, CH) for _ in range(H0)] for _ in range(SLOTS)]
        mminus = [[r.take(bf16, GJ0, CH) for _ in range(H0)] for _ in range(SLOTS)]
        small = [r.take(fp8, JP, CH) for _ in range(2)]
        s1bc0 = r.take(f32, H0, CH)
        stage0 = r.take(f32, IB, H0, 2 * PARTS * K0)
        r = Region(0, WORK, work)
        adj8 = [r.take(fp8, WIDE, JP, CH) for _ in range(SLOTS)]
        mask8 = [r.take(fp8, 2, WIDE, GJ1, CH) for _ in range(SLOTS)]
        s1bcA = [r.take(f32, CW) for _ in range(2)]
        s1bcD = r.take(f32, CW)
        stage1 = r.take(f32, IW, 3 * 2 * PARTS * K1)
        ep = r.take(f32, IW, 2, K1)
        ep2 = r.take(f32, IW, 2, K1)
        w0 = sb("w0", [P, H0, PARTS * K0], f32)
        flag0 = sb("flag0", [P, H0], f32)
        rec0 = sb("rec0", [P, H0], f32)
        x_in = sb("x_in", [P, IB, D], f32)
        r = Region(0, IB * D, x_in[:, :, :].rearrange("p i d -> p (i d)"))
        flag1 = r.take(f32, IW, 2)
        rec1 = r.take(f32, IW, 2)
        agg_sb = r.take(f32, IW, 2, HD1)
        FB = NB // 8 if NB >= 32 else NB // 4
        NF = NB // FB
        FS = 4
        r = Region(0, SLOTS * 2 * WIDE * JP * CH // 4, work)
        fin_y = [r.take(f32, FB, D) for _ in range(FS)]
        fin_h = [r.take(f32, FB, D) for _ in range(FS)]
        fin_x = [r.take(f32, FB, D) for _ in range(FS)]
        fin_e = [r.take(f32, FB, D) for _ in range(FS)]

        bank = [ctx.enter_context(nc.psum_tensor(f"bank{i}", [P, 512], f32)) for i in range(8)]

        def bc(ap, n):
            return ap.unsqueeze(len(ap.shape)).to_broadcast([*ap.shape, n])

        block = ctx.enter_context(nc.Block())
        sync, act, dve, pe, pool = nc.sync, nc.scalar, nc.vector, nc.tensor, nc.gpsimd
        phase_end = sem("phase_end")

        passed = {id(e): sem(f"passed_{n}") for n, e in (("sp", sync), ("act", act), ("dve", dve), ("pe", pe), ("pool", pool))}

        def wait_alone(eng, s, value):
            eng.wait_ge(s, value)
            eng.sem_inc(passed[id(eng)], 1)

        def phase_over(eng, k):
            eng.drain().then_inc(phase_end, 1)
            eng.wait_ge(phase_end, 5 * k)

        xv = x.rearrange("(b p) d -> p b d", p=P)
        x1v = x1_dram.rearrange("(b p) d -> p b d", p=P)
        h1v = h1_dram.rearrange("(b p) d -> p b d", p=P)
        LG = 8

        const_in = sem("const_in")
        w_in = [sem("w_in0"), sem("w_in1")]
        consts = sem("consts")
        weights_in_psum = sem("weights_in_psum")
        brow_ready = sem("brow_ready")
        bias_in_psum = sem("bias_in_psum")
        weights_ready = sem("weights_ready")
        HEADS = (H0, H1)

        def load_weights(eng, l):
            H, HD = (H0, HD0) if l == 0 else (H1, HD1)
            mats, biases = (((W1, W2), (b1, b2)) if l == 0 else ((Ww,), (Wb,)))
            for k in range(len(mats)):
                eng.dma_start(wn[l][k], mats[k]).then_inc(w_in[l], 16)
                eng.dma_start(bcol[l][k], biases[k].rearrange("(p o) -> p o", o=1)).then_inc(w_in[l], 16)
            eng.dma_start(wcat[l][:, 0:128], W3T if l == 0 else WwT).then_inc(w_in[l], 16)
            eng.dma_start(brow[l][0:1, 0:128], (b3 if l == 0 else Wb).rearrange("(o n) -> o n", o=1)).then_inc(w_in[l], 16)
            eng.wait_ge(consts, 1)
            for k in range(2):
                for h in range(H):
                    row = (a[h, k * HD:(k + 1) * HD] if l == 0 else aw[0, k * HD:(k + 1) * HD])
                    eng.dma_start(ablk[l][k][h * HD:(h + 1) * HD, h:h + 1],
                                  row.rearrange("(p o) -> p o", o=1)).then_inc(w_in[l], 16)
            if l == 1:
                eng.dma_start(abrow[0:1, 0:1], ab.rearrange("(o n) -> o n", o=1)).then_inc(w_in[l], 16)

        def weights_loaded(eng, l):
            eng.wait_ge(w_in[l], 16 * ((6 if l == 0 else 4) + 2 * HEADS[l] + (l == 1)))

        def weights_pe(l):
            H = HEADS[l]
            weights_loaded(pe, l)
            if l == 0:
                pe.wait_ge(const_in, 16)
            else:
                pe.wait_ge(weights_ready, 2)
            for n, k in enumerate((1, 0)):
                m = k if l == 0 else 0
                o = slice(n * H, (n + 1) * H)
                nc.tensor.matmul(bank[6][:, o], wn[l][m], ablk[l][k][:, 0:H], start=True, stop=True)
                last = nc.tensor.matmul(bank[7][0:1, o], bcol[l][m], ablk[l][k][:, 0:H], start=True, stop=l == 0 or n == 0)
            if l == 1:
                last = nc.tensor.matmul(bank[7][0:1, H:2 * H], ones[0:1, 0:1], abrow[0:1, 0:1].to_broadcast([1, H]),
                                        start=False, stop=True)
            last.then_inc(weights_in_psum, 1)
            pe.wait_ge(brow_ready, l + 1)
            VW = 128 + 2 * H
            nc.tensor.matmul(bank[7][:, 0:VW], ones[0:1, 0:P], brow[l][0:1, 0:VW], start=True, stop=True)
            nc.tensor.matmul(bank[6][0:2 * H, 64:65], brow[l][0:1, 128:VW], ones[0:1, 0:1],
                             start=True, stop=True).then_inc(bias_in_psum, 1)

        def weights_act(l):
            H = HEADS[l]
            VW = 128 + 2 * H
            act.wait_ge(weights_in_psum, l + 1)
            nc.scalar.copy(wcat[l][:, 128:VW], bank[6][:, 0:2 * H])
            nc.scalar.copy(brow[l][0:1, 128:VW], bank[7][0:1, 0:2 * H]).then_inc(brow_ready, 1)
            act.wait_ge(bias_in_psum, l + 1)
            nc.scalar.copy(ball[l][:, 0:VW], bank[7][:, 0:VW]).then_inc(weights_ready, 1)
            nc.scalar.copy(bias_col[l][0:2 * H, :], bank[6][0:2 * H, 64:65]).then_inc(weights_ready, 1)

        LB = NB // LG
        BT = LB // 4
        QB = NB // 4
        GQ = QB // XG

        class Prologue:
            def __init__(self, layer):
                self.l, self.s = layer, {}
                self.H, self.HD = (H0, HD0) if layer == 0 else (H1, HD1)
                self.K = self.HD + 1
                self.VW = 128 + 2 * self.H
                for name in ("mean_done",
                             "centred",
                             "squared",
                             "var_done",
                             "rstd_done",
                             "y_done",
                             "hT_in_psum",
                             "hT_copied",
                             "rows_in_psum",
                             "rows_copied",
                             "rows_stored",
                             "h_stored",
                             "max_found",
                             "max_in_psum",
                             "hsum_done",
                             "sumv_in_psum",
                             "sums_read",
                             "v_in_psum",
                             "v_copied",
                             "shifted",
                             "b_exp",
                             "ac_exp",
                             "xf_ready",
                             "hi_done", "rest1", "mid_done", "lo_done",
                             "dve_step"):
                    self.s[name] = sem(f"l{layer}_{name}")
                self.x_in = [sem(f"l{layer}_x_in{g}") for g in range(LG)]

            def views(self, b0, b1):
                H = self.H
                return V32[:, b0:b1, 0:128], V32[:, b0:b1, 128:128 + H], V32[:, b0:b1, 128 + H:128 + 2 * H]

        def xparts(p, g):
            w = p.H * 2 * PARTS * p.K
            v = Xt[:, g * XG * w:(g + 1) * XG * w]
            return v.rearrange("p (m t k) -> p m t k", t=PARTS, k=p.K)

        def xf_view(p, g):
            v = xf[g % XS][:, 0:XG * p.H * 2 * p.K]
            return v.rearrange("p (m k) -> p m k", k=p.K)

        def pro_sync(p):
            src = xv if p.l == 0 else x1v
            for g in range(LG):
                if p.l == 1 and g == LG - 1:
                    sync.wait_ge(x1_last, 16)
                sync.dma_start(x_all[:, g * LB:(g + 1) * LB, :], src[:, g * LB:(g + 1) * LB, :]).then_inc(p.x_in[g], 16)
            if p.l == 0:
                sync.dma_start(ident[:, :], ident_in).then_inc(const_in, 16)
                load_weights(sync, 1)
            else:
                for g in range(LG):
                    sync.wait_ge(p.s["y_done"], g + 1)
                    sync.dma_start(h1v[:, g * LB:(g + 1) * LB, :],
                                   x_all[:, g * LB:(g + 1) * LB, :]).then_inc(p.s["h_stored"], 16)
            sync.wait_ge(p.s["rows_copied"], N // 512)
            sync.dma_start(s1_rows[p.l], rows_sb[p.H:2 * p.H, :]).then_inc(p.s["rows_stored"], 16)
            sync.wait_ge(p.s["rows_stored"], 16)
            if p.l == 1:
                sync.wait_ge(p.s["h_stored"], 16 * LG)

        def pro_pool(p):
            H, HD, K = p.H, p.HD, p.K
            if p.l == 0:
                pool.memset(ones[:, :], 1.0)
                pool.memset(minus1[:, :], -1.0)
                pool.memset(minus_half[:, :], -0.5)
                for l in range(2):
                    for k in range(2):
                        pool.memset(ablk[l][k], 0.0)
                pool.memset(sumV[:, :], float(N)).then_inc(consts, 1)
                pool.wait_ge(consts, 1)
            for g in range(LG + 1):
                if g < LG:
                    s = slice(g * LB, (g + 1) * LB)
                    pool.wait_ge(p.s["mean_done"], g + 1)
                    pool.tensor_tensor(x_all[:, s, :], x_all[:, s, :], bc(stat[:, 0, s], D), ALU.subtract).then_inc(p.s["centred"], 1)
                if g >= 1:
                    s = slice((g - 1) * LB, g * LB)
                    pool.wait_ge(p.s["var_done"], g)
                    pool.tensor_tensor(stat[:, 1, s], stat[:, 1, s], minus_half[:, s], ALU.pow).then_inc(p.s["rstd_done"], 1)
            for g in range(4 * GQ):
                if g % GQ == 0:
                    pool.wait_ge(p.s["b_exp"], 4 * (g // GQ + 1))
                if g >= XS:
                    pool.wait_ge(p.s["lo_done"], g - XS + 1)
                bl = slice(g * XG, (g + 1) * XG)
                o = xf_view(p, g).rearrange("p (b h t) k -> p b h t k", h=H, t=2)
                Vv, _, _ = p.views(g * XG, (g + 1) * XG)
                for t in range(2):
                    pool.tensor_tensor(o[:, :, :, t, 0:HD], Vv.rearrange("p b (h d) -> p b h d", h=H),
                                       bc(bexp[:, bl, 0:H, t], HD), ALU.mult)
                pool.tensor_copy(o[:, :, :, :, HD], bexp[:, bl, 0:H, :]).then_inc(p.s["xf_ready"], 1)

        def pro_dve(p):
            H, HD, K = p.H, p.HD, p.K
            steps = [0]

            def chain(ins):
                steps[0] += 1
                ins.then_inc(p.s["dve_step"], 1)
                dve.wait_ge(p.s["dve_step"], steps[0])

            if p.l == 1:
                norm_last()
            for g in range(LG + 2):
                if g < LG:
                    s = slice(g * LB, (g + 1) * LB)
                    dve.wait_ge(p.x_in[g], 16)
                    chain(nc.vector.reduce_sum(stat[:, 0, s], x_all[:, s, :], axis=AX.X))
                    nc.vector.tensor_scalar(stat[:, 0, s], stat[:, 0, s], 1.0 / D, None, ALU.mult).then_inc(p.s["mean_done"], 1)
                if 1 <= g <= LG:
                    s = slice((g - 1) * LB, g * LB)
                    dve.wait_ge(p.s["squared"], g)
                    chain(nc.vector.reduce_sum(stat[:, 1, s], sq[:, s, :], axis=AX.X))
                    nc.vector.tensor_scalar(stat[:, 1, s], stat[:, 1, s], 1.0 / D, EPS, ALU.mult, ALU.add).then_inc(p.s["var_done"], 1)
                if g >= 2:
                    s = slice((g - 2) * LB, (g - 1) * LB)
                    dve.wait_ge(p.s["rstd_done"], g - 1)
                    nc.vector.tensor_tensor(x_all[:, s, :], x_all[:, s, :], bc(stat[:, 1, s], D), ALU.mult).then_inc(p.s["y_done"], 1)
            for q in range(4):
                dve.wait_ge(p.s["rows_copied"], (q + 1) * N // 2048)
                last = nc.vector.reduce_max(rowmax[0:2 * H, q:q + 1], rows_sb[0:2 * H, q * N // 4:(q + 1) * N // 4], axis=AX.X)
            chain(last)
            nc.vector.reduce_max(rowmax[0:2 * H, 4:5], rowmax[0:2 * H, 0:4], axis=AX.X).then_inc(p.s["max_found"], 1)
            nc.vector.reduce_sum(hsum[:, N // 512:N // 512 + 1], hsum[:, 0:N // 512], axis=AX.X).then_inc(p.s["hsum_done"], 1)
            dve.wait_ge(p.s["max_in_psum"], 1)
            chain(nc.vector.tensor_copy(Smax[:, 0:H], bank[6][:, 0:H]))
            dve.wait_ge(p.s["sumv_in_psum"], 1)
            if p.l == 1:
                chain(nc.vector.memset(sumV[:, :], float(N)))
            nc.vector.scalar_tensor_tensor(
                out=sumV[:, 0:H * K].rearrange("p (h k) -> p h k", k=K)[:, :, 0:HD],
                in0=ball[p.l][:, 0:128].rearrange("p (h d) -> p h d", d=HD), scalar=float(N),
                in1=bank[7][:, 0:128].rearrange("p (h d) -> p h d", d=HD), op0=ALU.mult, op1=ALU.add).then_inc(p.s["sums_read"], 1)

            def cut(q):
                for g in range(q * GQ, (q + 1) * GQ + (q == 3)):
                    if g < 4 * GQ:
                        o, xs = xf_view(p, g), xparts(p, g)
                        dve.wait_ge(p.s["hi_done"], g + 1)
                        nc.vector.tensor_tensor(o, o, xs[:, :, 0, :], ALU.subtract).then_inc(p.s["rest1"], 1)
                    if g >= 1:
                        o, xs = xf_view(p, g - 1), xparts(p, g - 1)
                        dve.wait_ge(p.s["mid_done"], g)
                        nc.vector.tensor_tensor(xs[:, :, 2, :], o, xs[:, :, 1, :], ALU.subtract).then_inc(p.s["lo_done"], 1)

            bias2 = ball[p.l][:, 0:p.VW].unsqueeze(1).to_broadcast([P, 2, p.VW])
            for q in range(4):
                for t in range(q * QB // 2, (q + 1) * QB // 2):
                    dve.wait_ge(p.s["v_in_psum"], t + 1)
                    nc.vector.tensor_tensor(V32[:, 2 * t:2 * t + 2, 0:p.VW],
                                            bank[t % 4][:, 0:2 * p.VW].rearrange("p (b n) -> p b n", b=2),
                                            bias2, ALU.add).then_inc(p.s["v_copied"], 1)
                dve.wait_ge(p.s["v_copied"], (q + 1) * QB // 2)
                bl = slice(q * QB, (q + 1) * QB)
                _, s2v, s1v = p.views(q * QB, (q + 1) * QB)
                S = Smax[:, 0:H].unsqueeze(1).to_broadcast([P, QB, H])
                z, m = zrow[:, bl, 0:H], mrow[:, bl, 0:H]
                nc.vector.tensor_tensor(dexp[:, bl, 0:H], s2v, S, ALU.subtract)
                chain(nc.vector.tensor_tensor(z, s1v, S, ALU.add))
                nc.vector.tensor_scalar(thr[:, bl, 0:H], s2v, -1.0, None, ALU.mult)
                nc.vector.tensor_scalar(steep_s2[:, bl, 0:H], s2v, STEEP, None, ALU.mult)
                chain(nc.vector.scalar_tensor_tensor(out=m, in0=z, scalar=SLOPE, in1=z, op0=ALU.mult, op1=ALU.max))
                nc.vector.scalar_tensor_tensor(out=Ci[:, bl, 0:H], in0=z, scalar=SLOPE, in1=m,
                                               op0=ALU.mult, op1=ALU.subtract)
                nc.vector.tensor_tensor(Ai[:, bl, 0:H], z, m, ALU.subtract).then_inc(p.s["shifted"], 1)
                if q >= 1:
                    cut(q - 1)
            cut(3)

        def pro_act(p):
            H, HD, K = p.H, p.HD, p.K
            if p.l == 0:
                load_weights(act, 0)

            def squares(g):
                s = slice(g * LB, (g + 1) * LB)
                act.wait_ge(p.s["centred"], g + 1)
                nc.scalar.activation(sq[:, s, :], x_all[:, s, :], ACT.Square).then_inc(p.s["squared"], 1)

            def transposed_out(g):
                for t in range(g * BT, (g + 1) * BT):
                    act.wait_ge(p.s["hT_in_psum"], t + 1)
                    nc.scalar.activation(hT[:, t * 512:(t + 1) * 512], bank[t % 4][:, :], ACT.Relu,
                                         accum_out=hsum[:, t:t + 1]).then_inc(p.s["hT_copied"], 1)

            def rows_out(g):
                for t in range(g * BT, (g + 1) * BT):
                    act.wait_ge(p.s["rows_in_psum"], t + 1)
                    nc.scalar.activation(rows_sb[0:2 * H, t * 512:(t + 1) * 512], bank[4 + t % 2][0:2 * H, :], ACT.Identity,
                                         bias=bias_col[p.l][0:2 * H, :]).then_inc(p.s["rows_copied"], 1)

            for g in range(LG + 4):
                if g < LG:
                    squares(g)
                if g == 2 and p.l == 0:
                    for l in range(2):
                        weights_act(l)
                if g == 3:
                    act.wait_ge(weights_ready, 4)
                if 3 <= g < LG + 3:
                    transposed_out(g - 3)
                if g >= 4:
                    rows_out(g - 4)

            def exps(q):
                bl = slice(q * QB, (q + 1) * QB)
                act.wait_ge(p.s["shifted"], q + 1)
                for e in range(2):
                    for t in range(2):
                        power = (t + e * p.l) % 2
                        nc.scalar.activation(bexp[:, bl, e:H:2, t], dexp[:, bl, e:H:2], ACT.Exp,
                                             scale=SLOPE if power else 1.0).then_inc(p.s["b_exp"], 1)
                for v in (Ai, Ci):
                    nc.scalar.activation(v[:, bl, 0:H], v[:, bl, 0:H], ACT.Exp).then_inc(p.s["ac_exp"], 1)

            def parts(q):
                for g in range(q * GQ, (q + 1) * GQ + (q == 3)):
                    if g < 4 * GQ:
                        act.wait_ge(p.s["xf_ready"], g + 1)
                        nc.scalar.copy(xparts(p, g)[:, :, 0, :], xf_view(p, g)).then_inc(p.s["hi_done"], 1)
                    if g >= 1:
                        act.wait_ge(p.s["rest1"], g)
                        nc.scalar.copy(xparts(p, g - 1)[:, :, 1, :], xf_view(p, g - 1)).then_inc(p.s["mid_done"], 1)

            act.wait_ge(p.s["rows_stored"], 16)
            exps(0)
            for q in range(4):
                if q < 3:
                    exps(q + 1)
                parts(q)

        def pro_pe(p):
            H, HD, K = p.H, p.HD, p.K
            if p.l == 0:
                pe.wait_ge(consts, 1)
                for l in range(2):
                    weights_pe(l)
                pe.wait_ge(weights_ready, 4)

            def transposes(g):
                pe.wait_ge(p.s["y_done"], g + 1)
                for t in range(g * BT, (g + 1) * BT):
                    if t >= 4:
                        pe.wait_ge(p.s["hT_copied"], t - 3)
                    for b in range(4):
                        last = nc.tensor.transpose(bank[t % 4][:, b * P:(b + 1) * P], x_all[:, 4 * t + b, :], ident[:, :])
                    last.then_inc(p.s["hT_in_psum"], 1)

            def rows(g):
                for t in range(g * BT, (g + 1) * BT):
                    pe.wait_ge(p.s["hT_copied"], t + 1)
                    if t >= 2:
                        pe.wait_ge(p.s["rows_copied"], t - 1)
                    nc.tensor.matmul(bank[4 + t % 2][0:2 * H, :], wcat[p.l][:, 128:p.VW], hT[:, t * 512:(t + 1) * 512],
                                     start=True, stop=True).then_inc(p.s["rows_in_psum"], 1)

            for g in range(LG + 1):
                if g < LG:
                    transposes(g)
                if g >= 1:
                    rows(g - 1)
            pe.wait_ge(p.s["max_found"], 1)
            nc.tensor.matmul(bank[6][:, 0:H], rowmax[0:2 * H, 4:5].to_broadcast([2 * H, P]), ident[0:2 * H, 0:H],
                             start=True, stop=True).then_inc(p.s["max_in_psum"], 1)
            pe.wait_ge(p.s["hsum_done"], 1)
            nc.tensor.matmul(bank[7][:, 0:128], hsum[:, N // 512:N // 512 + 1].to_broadcast([P, P]), wcat[p.l][:, 0:128],
                             start=True, stop=True).then_inc(p.s["sumv_in_psum"], 1)
            if p.l == 1:
                pe.wait_ge(p.s["h_stored"], 16 * LG)
            for t in range(NB // 2):
                if t >= 4:
                    pe.wait_ge(p.s["v_copied"], t - 3)
                for b in range(2):
                    last = nc.tensor.matmul(bank[t % 4][:, b * p.VW:(b + 1) * p.VW], hT[:, (2 * t + b) * P:(2 * t + b + 1) * P],
                                            wcat[p.l][:, 0:p.VW], start=True, stop=True)
                last.then_inc(p.s["v_in_psum"], 1)

        x1_last = sem("x1_last")
        last_step = sem("last_step")
        x1_done = sem("x1_done")

        def norm_last():
            n = [0]

            def chain(ins):
                n[0] += 1
                ins.then_inc(last_step, 1)
                dve.wait_ge(last_step, n[0])

            st = stage0.rearrange("p i h (t k) -> p i h t k", t=2)
            for t, v in enumerate((Ai, Ci)):
                last = nc.vector.tensor_tensor(st[:, :, :, t, :], st[:, :, :, t, :],
                                               bc(v[:, NB - IB:NB, 0:H0], PARTS * K0), ALU.mult)
            chain(last)
            m = stage0.rearrange("p i h (t k) -> p (i h) t k", t=2 * PARTS)
            k3 = stage0.rearrange("p i h (t k) -> p (i h) t k", t=2)
            chain(nc.vector.tensor_tensor(k3[:, :, 0, :], k3[:, :, 0, :], k3[:, :, 1, :], ALU.add))
            for t in (1, 2):
                chain(nc.vector.tensor_tensor(m[:, :, 0, :], m[:, :, 0, :], m[:, :, t, :], ALU.add))
            flag = stage0.rearrange("p i h k -> p (i h) k")[:, :, 2 * K0:2 * K0 + 1]
            chain(nc.vector.tensor_scalar(flag, m[:, :, 0, HD0:K0], 0.0, None, ALU.is_equal))
            sv = sumV[:, 0:H0 * K0].rearrange("p (h k) -> p h k", k=K0)
            for i in range(IB):
                last = nc.vector.tensor_tensor(m[:, H0 * i:H0 * (i + 1), 1, :], sv,
                                               flag[:, H0 * i:H0 * (i + 1), :].to_broadcast([P, H0, K0]), ALU.mult)
            chain(last)
            chain(nc.vector.tensor_tensor(m[:, :, 0, :], m[:, :, 0, :], m[:, :, 1, :], ALU.add))
            chain(nc.vector.reciprocal(flag, m[:, :, 0, HD0:K0]))
            chain(nc.vector.tensor_tensor(m[:, :, 0, 0:HD0], m[:, :, 0, 0:HD0], flag.to_broadcast([P, IB * H0, HD0]), ALU.mult))
            dve.wait_ge(x_chunk_in, 16 * NCH)
            xm = x_in[:, :, :].rearrange("p i (h d) -> p (i h) d", h=H0)
            nc.vector.tensor_tensor(xm, xm, m[:, :, 0, 0:HD0], ALU.add).then_inc(x1_done, 1)

        def store_last():
            act.wait_ge(x1_done, 1)
            act.dma_start(x1chunk[NCH - 1], x_in[:, :, :]).then_inc(x1_last, 16)

        pro = [Prologue(0), Prologue(1)]

        adj_v = adj.rearrange("(c i p) (q j) -> c q p i j", i=IB, p=P, j=JP * P)
        xchunk = x.rearrange("(c i p) d -> c p i d", i=IB, p=P)
        x1chunk = x1_dram.rearrange("(c i p) d -> c p i d", i=IB, p=P)
        s1row0 = s1_rows[0].rearrange("h (c n) -> c h n", n=CH)
        nat_in = [sem(f"nat_in{s}") for s in range(S0)]
        transposed = [sem(f"transposed{s}") for s in range(S0)]
        shrunk = [sem(f"shrunk{s}") for s in range(S0)]
        mask_stored = [sem(f"mask_stored{s}") for s in range(2)]
        s1bc_in = [sem(f"s1bc_in{h}") for h in range(H0)]
        side_ready0 = [sem(f"side_ready0_{h}") for h in range(H0)]
        plus_ready0 = sem("plus_ready0")
        minus_ready0 = sem("minus_ready0")
        masks_free0 = sem("masks_free0")
        sums_ready0 = sem("sums_ready0")
        bank_free0 = [sem("bank_free0_act"), sem("bank_free0_dve")]
        stage_free0 = sem("stage_free0")
        x_chunk_in = sem("x_chunk_in")
        x1_ready = sem("x1_ready")
        x1_stored = sem("x1_stored")
        pool_step0 = sem("pool_step0")
        X0 = Xt[:, 0:NB * H0 * 2 * PARTS * K0].rearrange("p (b h t k) -> p b h t k", h=H0, t=2, k=PARTS * K0)

        def at(c, per, k):
            return c * per + k

        def side0(c, k, h):
            act.wait_ge(masks_free0, at(c, NG0, k + 1))
            for j in range(GJ0):
                last = nc.scalar.activation(mplus[k % SLOTS][h][:, j, :], s1bc0[:, h, :], ACT.Sigmoid, scale=STEEP,
                                            bias=steep_s2[:, k * GJ0 + j, h:h + 1])
            last.then_inc(side_ready0[h], 1)

        def s1_load0(c, h):
            act.dma_start(s1bc0[:, h, :], s1row0[c, h].unsqueeze(0).to_broadcast([P, CH])).then_inc(s1bc_in[h], 16)

        def copy_out0(c, who):
            eng, copy = (act, nc.scalar.copy) if who == 0 else (dve, nc.vector.tensor_copy)
            eng.wait_ge(stage_free0, at(c, IB, IB))
            for n in range(4):
                i, h = 2 * who + n // 2, n % 2
                if 4 * who + n < 7:
                    eng.wait_ge(sums_ready0, at(c, 7, 4 * who + n + 1))
                else:
                    eng.wait_ge(masks_free0, at(c, NG0, NG0 + SLOTS))
                copy(stage0[:, i, h, :], bank[4 * who + n][:, 0:2 * PARTS * K0]).then_inc(bank_free0[who], 1)

        def main0_act():
            act.sem_inc(bank_free0[0], 4)
            for h in range(H0):
                s1_load0(0, h)
            for h in range(H0):
                act.wait_ge(s1bc_in[h], 16)
                for k in range(AHEAD0):
                    side0(0, k, h)

            def chunk(c, more):
                for k in range(AHEAD0, NG0 - 2):
                    for h in range(H0):
                        side0(c, k, h)
                for h in range(H0):
                    for k in range(NG0 - 2, NG0):
                        side0(c, k, h)
                    if more:
                        act.wait_ge(side_ready0[h], at(c, NG0, NG0))
                        s1_load0(c + 1, h)
                if more:
                    for h in range(H0):
                        act.wait_ge(s1bc_in[h], at(c, 16, 32))
                        for k in range(AHEAD0):
                            side0(c + 1, k, h)
                copy_out0(c, 0)

            with act.Fori(0, NCH - 1) as c:
                chunk(c, True)
            chunk(NCH - 1, False)

        def masks0(c, k):
            q, half = k * GJ0 // JP, k * GJ0 % JP
            if half == 0:
                dve.wait_ge(transposed[q % S0], at(c, 64 * NP // S0, 64 * (q // S0 + 1)))
            m0 = adjT[q % S0][:, half:half + GJ0, :]
            for h in range(H0):
                dve.wait_ge(side_ready0[h], at(c, NG0, k + 1))
                m = mplus[k % SLOTS][h]
                nc.vector.tensor_tensor(m, m, m0, ALU.mult).then_inc(plus_ready0, 1)
            for h in range(H0):
                dve.wait_ge(plus_ready0, at(c, 2 * NG0, 2 * k + h + 1))
                nc.vector.tensor_tensor(mminus[k % SLOTS][h], m0, mplus[k % SLOTS][h], ALU.subtract).then_inc(minus_ready0, 1)

        def main0_dve():
            dve.sem_inc(bank_free0[1], 4)
            for k in range(AHEAD0):
                masks0(0, k)

            def chunk(c, more):
                for k in range(AHEAD0, NG0):
                    masks0(c, k)
                if more:
                    for k in range(AHEAD0):
                        masks0(c + 1, k)
                copy_out0(c, 1)

            with dve.Fori(0, NCH - 1) as c:
                chunk(c, True)
            chunk(NCH - 1, False)

        def main0_pe():
            pe.sem_inc(masks_free0, SLOTS)
            with pe.Fori(0, NCH) as c:
                for k in range(NG0):
                    pe.wait_ge(plus_ready0, at(c, 2 * NG0, 2 * k + 2))
                    pe.wait_ge(minus_ready0, at(c, 2 * NG0, 2 * k + 2))
                    for j in range(GJ0):
                        b = k * GJ0 + j
                        for i in range(IB):
                            for h in range(H0):
                                n = 2 * i + h
                                if b == 0:
                                    pe.wait_ge(bank_free0[n // 4], at(c, 4, n % 4 + 1))
                                for t, m in enumerate((mplus, mminus)):
                                    last = nc.tensor.matmul(
                                        bank[n][:, t * PARTS * K0:(t + 1) * PARTS * K0],
                                        m[k % SLOTS][h][:, j, i * P:(i + 1) * P], X0[:, b, h, t, :],
                                        start=b == 0 and t == 0, stop=b == NB - 1 and t == 1, skip_group_check=True)
                                if b == NB - 1 and n < 7:
                                    last.then_inc(sums_ready0, 1)
                    last.then_inc(masks_free0, 1)

        def main0_sync():
            def piece(c, q, first):
                s = q % S0
                wait_alone(sync, nat_in[s], at(c, 16 * NP // S0, 16 * (q // S0 + 1)))
                if not (first and q < S0):
                    wait_alone(sync, minus_ready0, at(c, 2 * NG0, 2 * (q - S0 + 1) * JP // GJ0))
                    wait_alone(sync, shrunk[s], at(c, 16 * NP // S0, 16 * (q // S0)))
                for i in range(IB):
                    sync.dma_start_transpose(adjT[s][:, :, i * P:(i + 1) * P], nat[s][:, i, :]).then_inc(transposed[s], 16)

            def store(c, q):
                wait_alone(sync, shrunk[q % S0], at(c, 16 * NP // S0, 16 * (q // S0 + 1)))
                sync.dma_start(adjT8[c, q], small[q % 2].rearrange("p j n -> p (j n)").bitcast(u8)).then_inc(mask_stored[q % 2], 16)

            for q in range(NP):
                piece(0, q, True)
                if q >= 2:
                    store(0, q - 2)
            with sync.Fori(1, NCH) as c:
                for q in range(NP):
                    piece(c, q, False)
                    if q < 2:
                        store(c - 1, NP + q - 2)
                    else:
                        store(c, q - 2)
            for q in (NP - 2, NP - 1):
                store(NCH - 1, q)
            for s in range(2):
                sync.wait_ge(mask_stored[s], 16 * NCH * NP // 2)

        EARLY0 = min(S0, NB * P // (IB * JP * P // 2))

        def early0_pool():
            pool.wait_ge(pro[0].s["v_in_psum"], NB // 2)
            for q in range(EARLY0):
                pool.dma_start(nat[q], adj_v[0, q]).then_inc(nat_in[q], 16)

        def main0_pool():
            def load(c, q, first):
                s = q % S0
                if not (first and q < S0):
                    wait_alone(pool, transposed[s], at(c, 64 * NP // S0, 64 * (q // S0)))
                pool.dma_start(nat[s], adj_v[c, q]).then_inc(nat_in[s], 16)

            def shrink(c, q, first):
                s = q % S0
                wait_alone(pool, transposed[s], at(c, 64 * NP // S0, 64 * (q // S0 + 1)))
                if not (first and q < 2):
                    wait_alone(pool, mask_stored[q % 2], at(c, 16 * NP // 2, 16 * (q // 2)))
                pool.dma_start(small[q % 2], adjT[s]).then_inc(shrunk[s], 16)

            def norm(c, i):
                n = [0]

                def chain(ins):
                    n[0] += 1
                    ins.then_inc(pool_step0, 1)
                    wait_alone(pool, pool_step0, at(c, 10 * IB, 10 * i + n[0]))

                if i == 0:
                    pool.dma_start(x_in[:, :, :], xchunk[c]).then_inc(x_chunk_in, 16)
                for who in range(2):
                    if i == 2 * who:
                        wait_alone(pool, bank_free0[who], at(c, 4, 8))
                bi = c * IB + i
                st = stage0[:, i, :, :].rearrange("p h (t k) -> p h t k", t=2)
                plus, minus = st[:, :, 0, :], st[:, :, 1, :]
                A = bc(Ai[:, bass.ds(bi, 1), 0:H0].rearrange("p o h -> p (o h)"), PARTS * K0)
                C = bc(Ci[:, bass.ds(bi, 1), 0:H0].rearrange("p o h -> p (o h)"), PARTS * K0)
                pool.tensor_tensor(plus, plus, A, ALU.mult)
                chain(pool.tensor_tensor(minus, minus, C, ALU.mult))
                chain(pool.tensor_tensor(w0[:, :, :], plus, minus, ALU.add))
                pool.sem_inc(stage_free0, 1)
                chain(pool.tensor_tensor(w0[:, :, 0:K0], w0[:, :, 0:K0], w0[:, :, K0:2 * K0], ALU.add))
                chain(pool.tensor_tensor(w0[:, :, 0:K0], w0[:, :, 0:K0], w0[:, :, 2 * K0:3 * K0], ALU.add))
                chain(pool.tensor_scalar(flag0[:, :], w0[:, :, HD0], 0.0, None, ALU.is_equal))
                chain(pool.tensor_tensor(w0[:, :, K0:2 * K0], sumV[:, 0:H0 * K0].rearrange("p (h k) -> p h k", k=K0),
                                         bc(flag0[:, :], K0), ALU.mult))
                chain(pool.tensor_tensor(w0[:, :, 0:K0], w0[:, :, 0:K0], w0[:, :, K0:2 * K0], ALU.add))
                chain(pool.tensor_tensor(rec0[:, :], w0[:, :, HD0], minus1[:, 0:H0], ALU.pow))
                chain(pool.tensor_tensor(w0[:, :, 0:HD0], w0[:, :, 0:HD0], bc(rec0[:, :], HD0), ALU.mult))
                if i == 0:
                    wait_alone(pool, x_chunk_in, at(c, 16, 16))
                chain(pool.tensor_tensor(x_in[:, i, :].rearrange("p (h d) -> p h d", h=H0),
                                         x_in[:, i, :].rearrange("p (h d) -> p h d", h=H0), w0[:, :, 0:HD0], ALU.add))
                if i == IB - 1:
                    pool.dma_start(x1chunk[c], x_in[:, :, :]).then_inc(x1_stored, 16)
                    wait_alone(pool, x1_stored, at(c, 16, 16))

            when = [min(NP // IB * (i + 1), NP - 1) for i in range(IB)]

            def chunk(c, first):
                for q in range(NP):
                    if not (first and q < EARLY0):
                        load(c, q, first)
                    if q >= 2:
                        shrink(c, q - 2, first)
                    elif not first:
                        shrink(c - 1, NP + q - 2, False)
                    for i in range(IB):
                        if not first and when[i] == q:
                            norm(c - 1, i)

            pool.sem_inc(stage_free0, IB)
            chunk(0, True)
            with pool.Fori(1, NCH) as c:
                chunk(c, False)
            for q in (NP - 2, NP - 1):
                shrink(NCH - 1, q, False)
            pool.dma_start(x_in[:, :, :], xchunk[NCH - 1]).then_inc(x_chunk_in, 16)
            pool.wait_ge(x_chunk_in, 16 * NCH)
            pool.wait_ge(x1_stored, 16 * (NCH - 1))

        adj8_v = adjT8.rearrange("(c a) q p n -> c q p a n", a=WIDE)
        s1row1 = s1_rows[1].rearrange("h (c n) -> c h n", n=CW)
        aggchunk = agg_dram.rearrange("(c i p) (h d) -> c p i h d", i=IW, p=P, d=HD1)
        X1 = Xt[:, 0:NB * H1 * 2 * PARTS * K1].rearrange("p (b k) -> p b k", b=NB)
        M1 = 2 * PARTS * K1
        PER_GROUP = JP // GJ1
        s1A_in = sem("s1A_in")
        s1D_in = sem("s1D_in")
        adj_in = [sem(f"adj_in{s}") for s in range(SLOTS)]
        side_act = sem("side_act")
        side_dve = sem("side_dve")
        mask_ready = sem("mask_ready")
        masks_free = sem("masks_free")
        sums_ready = sem("sums_ready")
        bank_free = sem("bank_free")
        stage_free = sem("stage_free")
        agg_step = sem("agg_step")
        agg_stored = sem("agg_stored")

        class Sweep:
            def __init__(self, w):
                self.w, self.h = w, 2 * w
                self.c0, self.c1 = w * NW, (w + 1) * NW

        sweeps = [Sweep(w) for w in range(H1 // 2)]

        def sweep_loops(eng, chunk):
            for n, w in enumerate(sweeps):
                with eng.Fori(w.c0, w.c1 - 1) as c:
                    chunk(w, c, (w, c + 1))
                chunk(w, w.c1 - 1, (sweeps[n + 1], w.c1) if n + 1 < len(sweeps) else None)

        def pair_loops(eng, chunk):
            for n, w in enumerate(sweeps):
                with eng.Fori(0, NW // 2 - 1) as pair:
                    c = pair * 2 + w.c0
                    chunk(w, c, 0, (w, c + 1))
                    chunk(w, c + 1, 1, (w, c + 2))
                chunk(w, w.c1 - 2, 0, (w, w.c1 - 1))
                chunk(w, w.c1 - 1, 1, (sweeps[n + 1], w.c1) if n + 1 < len(sweeps) else None)

        def s1_load(w, c, who, slot=0):
            eng, dst, done = ((act, s1bcA[slot], s1A_in), (sync, s1bcD, s1D_in))[who]
            eng.dma_start(dst, s1row1[c - w.c0, w.h + who].unsqueeze(0).to_broadcast([P, CW])).then_inc(done, 16)

        def side1_act(w, c, k, slot):
            wait_alone(act, masks_free, at(c, NG1, k + 1))
            if k == SHARED[0]:
                wait_alone(act, s1D_in, at(c, 16, 16))
            blocks = [(0, j) for j in range(GJ1)] + ([(1, GJ1 - 1)] if k in SHARED else [])
            for h, j in blocks:
                s1 = (s1bcA[slot], s1bcD)[h].rearrange("p (a n) -> p a n", a=WIDE)
                last = nc.scalar.activation(mask8[k % SLOTS][:, h, :, j, :], s1, ACT.Sigmoid, scale=STEEP,
                                            bias=steep_s2[:, k * GJ1 + j, w.h + h:w.h + h + 1], saturate=False)
            last.then_inc(side_act, 1)

        def copy_out1(w, c):
            wait_alone(act, stage_free, at(c, 1, 1))
            for b in range(IW):
                if b < IW - 1:
                    wait_alone(act, sums_ready, at(c, IW - 1, b + 1))
                else:
                    wait_alone(act, masks_free, at(c, NG1, NG1 + SLOTS))
                nc.scalar.copy(stage1[:, b, :], bank[b][:, 0:3 * M1]).then_inc(bank_free, 1)

        def main1_act():
            act.sem_inc(bank_free, IW)
            s1_load(sweeps[0], 0, 0)
            act.wait_ge(s1A_in, 16)
            for k in range(AHEAD):
                side1_act(sweeps[0], 0, k, 0)

            def chunk(w, c, slot, following):
                for k in range(AHEAD, NG1):
                    side1_act(w, c, k, slot)
                    if k == AHEAD and following:
                        wait_alone(act, side_act, at(c, NG1, AHEAD))
                        s1_load(*following, 0, 1 - slot)
                if following:
                    wait_alone(act, s1A_in, at(c, 16, 32))
                    for k in range(AHEAD):
                        side1_act(*following, k, 1 - slot)
                copy_out1(w, c)

            pair_loops(act, chunk)

        def masks1(w, c, k):
            wait_alone(dve, masks_free, at(c, NG1, k + 1))
            for j in range(GJ1 - (k in SHARED)):
                last = nc.vector.tensor_scalar(mask8[k % SLOTS][:, 1, :, j, :], s1bcD.rearrange("p (a n) -> p a n", a=WIDE),
                                               thr[:, k * GJ1 + j, w.h + 1:w.h + 2], None, ALU.is_ge, saturate=False)
            last.then_inc(side_dve, 1)
            q, part = k // PER_GROUP, k % PER_GROUP
            if part == 0:
                wait_alone(dve, adj_in[q % SLOTS], at(c, 16 * NP // SLOTS, 16 * (q // SLOTS + 1)))
            m0 = adj8[q % SLOTS][:, :, part * GJ1:(part + 1) * GJ1, :].rearrange("p a j n -> p a (j n)").bitcast(i32)
            for n in range(2):
                wait_alone(dve, (side_act, side_dve)[n], at(c, NG1, k + 1))
                m = mask8[k % SLOTS][:, n, :, :, :].rearrange("p a j n -> p a (j n)").bitcast(i32)
                nc.vector.tensor_tensor(m, m, m0, ALU.bitwise_and).then_inc(mask_ready, 1)

        def main1_dve():
            dve.wait_ge(s1D_in, 16)
            for k in range(AHEAD):
                masks1(sweeps[0], 0, k)

            def chunk(w, c, slot, following):
                for k in range(AHEAD, NG1):
                    masks1(w, c, k)
                if following:
                    wait_alone(dve, s1D_in, at(c, 16, 32))
                    for k in range(AHEAD):
                        masks1(*following, k)

            pair_loops(dve, chunk)

        def main1_pe():
            pe.sem_inc(masks_free, SLOTS)

            def group(w, c, k):
                wait_alone(pe, mask_ready, at(c, 2 * NG1, 2 * (k + 1)))
                q, part = k // PER_GROUP, k % PER_GROUP
                for j in range(GJ1):
                    b = k * GJ1 + j
                    for i in range(IW):
                        half, cols = i // IB, slice(i % IB * P, (i % IB + 1) * P)
                        if b == 0:
                            wait_alone(pe, bank_free, at(c, IW, i + 1))
                        for n in range(3):
                            if n < 2:
                                mask, o = mask8[k % SLOTS][:, n, half, j, cols], (w.h + n) * M1
                            else:
                                mask, o = adj8[q % SLOTS][:, half, part * GJ1 + j, cols], w.h * M1 + M1 // 2
                            last = nc.tensor.matmul(bank[i][:, n * M1:(n + 1) * M1], mask, X1[:, b, o:o + M1],
                                                    start=b == 0 and n == 0, stop=b == NB - 1 and n == 2,
                                                    skip_group_check=True)
                        if b == NB - 1 and i < IW - 1:
                            last.then_inc(sums_ready, 1)
                last.then_inc(masks_free, 1)

            for k in range(AHEAD):
                group(sweeps[0], 0, k)

            def chunk(w, c, following):
                for k in range(AHEAD, NG1):
                    group(w, c, k)
                if following:
                    for k in range(AHEAD):
                        group(*following, k)

            sweep_loops(pe, chunk)

        EARLY1 = min(SLOTS, NB * P // (WIDE * JP * CH // 4))

        def early1_sync():
            sync.wait_ge(pro[1].s["v_in_psum"], NB // 2)
            for q in range(EARLY1):
                sync.dma_start(adj8[q].rearrange("p a j n -> p a (j n)").bitcast(u8), adj8_v[0, q]).then_inc(adj_in[q], 16)

        def main1_sync():
            def chunk(w, c, first):
                for q in range(NP):
                    s = q % SLOTS
                    if first and q < EARLY1:
                        continue
                    if not (first and q < SLOTS):
                        wait_alone(sync, masks_free, at(c, NG1, (q - SLOTS + 1) * PER_GROUP + SLOTS))
                    sync.dma_start(adj8[s].rearrange("p a j n -> p a (j n)").bitcast(u8), adj8_v[c - w.c0, q]).then_inc(adj_in[s], 16)
                    if q == 1 and not first:
                        wait_alone(sync, side_dve, at(c, NG1, 0))
                        wait_alone(sync, side_act, at(c, NG1, 0))
                        s1_load(w, c, 1)

            s1_load(sweeps[0], 0, 1)
            chunk(sweeps[0], 0, True)
            for w in sweeps:
                with sync.Fori(max(w.c0, 1), w.c1) as c:
                    chunk(w, c, False)

        def main1_pool():
            pool.sem_inc(stage_free, 1)
            st = stage1.rearrange("p i (s t k) -> p i s t k", s=6, t=PARTS)
            s3 = stage1.rearrange("p i (s k) -> p i s k", s=6)
            for w in sweeps:
                with pool.Fori(w.c0, w.c1) as c:
                    n = [0]

                    def chain(ins):
                        n[0] += 1
                        ins.then_inc(agg_step, 1)
                        wait_alone(pool, agg_step, at(c, 11, n[0]))

                    wait_alone(pool, bank_free, at(c, IW, 2 * IW))
                    chain(pool.tensor_tensor(s3[:, :, 1:3, :], s3[:, :, 4:6, :], s3[:, :, 1:3, :], ALU.subtract))
                    for t in (1, 2):
                        chain(pool.tensor_tensor(st[:, :, 0:4, 0, :], st[:, :, 0:4, 0, :], st[:, :, 0:4, t, :], ALU.add))
                    for src, dst, sect in ((Ai, ep, (0, 3)), (Ci, ep2, (1, 2))):
                        scale = src[:, bass.ds((c - w.c0) * IW, IW), w.h:w.h + 2]
                        for h in range(2):
                            last = pool.tensor_tensor(dst[:, :, h, :], st[:, :, sect[h], 0, :], bc(scale[:, :, h], K1), ALU.mult)
                        chain(last)
                    pool.sem_inc(stage_free, 1)
                    chain(pool.tensor_tensor(ep, ep, ep2, ALU.add))
                    chain(pool.tensor_scalar(flag1, ep[:, :, :, HD1], 0.0, None, ALU.is_equal))
                    for h in range(2):
                        v = sumV[:, (w.h + h) * K1:(w.h + h + 1) * K1].unsqueeze(1).to_broadcast([P, IW, K1])
                        last = pool.tensor_tensor(ep2[:, :, h, :], v, bc(flag1[:, :, h], K1), ALU.mult)
                    chain(last)
                    chain(pool.tensor_tensor(ep, ep, ep2, ALU.add))
                    chain(pool.tensor_tensor(rec1, ep[:, :, :, HD1], minus1[:, 0:IW * 2].rearrange("p (i h) -> p i h", h=2), ALU.pow))
                    chain(pool.tensor_tensor(agg_sb, ep[:, :, :, 0:HD1], bc(rec1, HD1), ALU.mult))
                    pool.dma_start(aggchunk[c - w.c0][:, :, w.h:w.h + 2, :].rearrange("p i h d -> p i (h d)"),
                                   agg_sb.rearrange("p i h d -> p i (h d)")).then_inc(agg_stored, 16)
                    wait_alone(pool, agg_stored, at(c, 16, 16))

        aggv = agg_dram.rearrange("(b p) d -> p b d", p=P)
        outv = out.rearrange("(b p) d -> p b d", p=P)
        fin_in = [sem(f"fin_in{s}") for s in range(FS)]
        fin_low = sem("fin_low")
        fin_exp = sem("fin_exp")
        fin_done = sem("fin_done")
        fin_sum = sem("fin_sum")
        fin_two = sem("fin_two")
        out_stored = [sem(f"out_stored{s}") for s in range(FS)]

        CF = FB * P

        def fin_sync():
            def load(t):
                s = t % FS
                if t >= FS:
                    sync.wait_ge(fin_done, t - FS + 1)
                for dst, src in ((fin_h, h1v), (fin_x, x1v)):
                    sync.dma_start(dst[s], src[:, t * FB:(t + 1) * FB, :]).then_inc(fin_in[s], 16)
                sync.wait_ge(agg_stored, 16 * (sweeps[-1].c0 + -(-(t + 1) * CF // CW)))
                sync.dma_start(fin_y[s], aggv[:, t * FB:(t + 1) * FB, :]).then_inc(fin_in[s], 16)

            def store(t):
                sync.wait_ge(fin_done, t + 1)
                sync.dma_start(outv[:, t * FB:(t + 1) * FB, :], fin_e[t % FS]).then_inc(out_stored[t % FS], 16)

            sync.wait_ge(masks_free, SLOTS + sweeps[-1].c1 * NG1)
            for t in range(NF):
                load(t)
                if t >= FS - 1:
                    store(t - FS + 1)
            for t in range(NF - FS + 1, NF):
                store(t)
            for s in range(FS):
                sync.wait_ge(out_stored[s], 16 * NF // FS)

        def fin_dve():
            def first(t):
                s = t % FS
                dve.wait_ge(fin_in[s], 48 * (t // FS + 1))
                nc.vector.scalar_tensor_tensor(out=fin_y[s], in0=fin_h[s], scalar=0.0, in1=fin_y[s],
                                               op0=ALU.max, op1=ALU.add).then_inc(fin_sum, 1)
                dve.wait_ge(fin_sum, t + 1)
                nc.vector.tensor_scalar(fin_h[s], fin_y[s], 0.0, None, ALU.min).then_inc(fin_low, 1)

            def second(t):
                s = t % FS
                dve.wait_ge(fin_exp, t + 1)
                nc.vector.scalar_tensor_tensor(out=fin_y[s], in0=fin_y[s], scalar=0.0, in1=fin_e[s],
                                               op0=ALU.max, op1=ALU.add).then_inc(fin_two, 1)
                dve.wait_ge(fin_two, t + 1)
                nc.vector.scalar_tensor_tensor(out=fin_e[s], in0=fin_y[s], scalar=-1.0, in1=fin_x[s],
                                               op0=ALU.add, op1=ALU.add).then_inc(fin_done, 1)

            for t in range(NF + 1):
                if t < NF:
                    first(t)
                if t >= 1:
                    second(t - 1)

        def fin_act():
            for t in range(NF):
                act.wait_ge(fin_low, t + 1)
                if t >= FS:
                    act.wait_ge(out_stored[t % FS], 16 * (t // FS))
                nc.scalar.activation(fin_e[t % FS], fin_h[t % FS], ACT.Exp).then_inc(fin_exp, 1)

        @block.sync
        def _(eng):
            pro_sync(pro[0])
            phase_over(eng, 1)
            main0_sync()
            phase_over(eng, 2)
            pro_sync(pro[1])
            early1_sync()
            phase_over(eng, 3)
            main1_sync()
            fin_sync()

        @block.scalar
        def _(eng):
            pro_act(pro[0])
            phase_over(eng, 1)
            main0_act()
            phase_over(eng, 2)
            store_last()
            pro_act(pro[1])
            phase_over(eng, 3)
            main1_act()
            fin_act()

        @block.vector
        def _(eng):
            pro_dve(pro[0])
            phase_over(eng, 1)
            main0_dve()
            phase_over(eng, 2)
            pro_dve(pro[1])
            phase_over(eng, 3)
            main1_dve()
            fin_dve()

        @block.tensor
        def _(eng):
            pro_pe(pro[0])
            phase_over(eng, 1)
            main0_pe()
            phase_over(eng, 2)
            pro_pe(pro[1])
            phase_over(eng, 3)
            main1_pe()

        @block.gpsimd
        def _(eng):
            pro_pool(pro[0])
            early0_pool()
            phase_over(eng, 1)
            main0_pool()
            phase_over(eng, 2)
            pro_pool(pro[1])
            phase_over(eng, 3)
            main1_pool()


def kernel(**inputs):
    import numpy as np
    import concourse.bacc as bacc
    from concourse import mybir
    from concourse.bass_utils import run_bass_kernel_spmd as run

    i = {k: np.ascontiguousarray(v) for k, v in inputs.items()}
    arrays = {
        "x": i["x"], "adj": i["adj"],
        "W1": i["L0_gnn_W1"], "b1": i["L0_gnn_b1"], "W2": i["L0_gnn_W2"], "b2": i["L0_gnn_b2"],
        "W3": i["L0_gnn_W3"], "W3T": np.ascontiguousarray(i["L0_gnn_W3"].T), "b3": i["L0_gnn_b3"], "a": i["L0_gnn_a"],
        "Ww": i["L1_gnn_W_w"], "WwT": np.ascontiguousarray(i["L1_gnn_W_w"].T), "Wb": i["L1_gnn_W_b"],
        "aw": i["L1_gnn_a_w"], "ab": i["L1_gnn_a_b"],
        "ident": np.eye(128, dtype=np.float32),
    }
    nc = bacc.Bacc("TRN2", target_bir_lowering=False, num_devices=1)
    args = [nc.dram_tensor(f"in_{n}", v.shape, mybir.dt.from_np(v.dtype), kind="ExternalInput").ap()
            for n, v in arrays.items()]
    out = nc.dram_tensor("out_0", i["x"].shape, mybir.dt.float32, kind="ExternalOutput").ap()
    gat_kernel(nc, *args, out)
    r = run(nc, [{f"in_{n}": v for n, v in arrays.items()}], core_ids=[0])
    return r.results[0]["out_0"]
```
